# Optimizing a Trainium2 kernel written in Bass

```python
import numpy as np
import jax
import jax.numpy as jnp

def _softmax(x, axis=-1):
    return jax.nn.softmax(x, axis=axis)

def _gelu(x):
    return jax.nn.gelu(x, approximate=True)

def _silu(x):
    return jax.nn.silu(x)

def _sigmoid(x):
    return jax.nn.sigmoid(x)

def _layernorm(x, axis=-1, eps=1e-05):
    m = jnp.mean(x, axis=axis, keepdims=True)
    v = jnp.var(x, axis=axis, keepdims=True)
    return (x - m) / jnp.sqrt(v + eps)

def _scatter_add(tgt, idx, src, axis=0):
    return tgt.at[idx].add(src)

def _segment_sum(src, seg, n):
    return jax.ops.segment_sum(src, seg, n)
kernel_name = 'mk_flamingo_gated_d2_seqx_r8_9fe5d6'

def setup_inputs(seed: int=0):
    np.random.seed(seed)
    _w = jnp.asarray

    def _rec_inputs():
        import jax
        import jax.numpy as jnp
        _rk = jax.random.key(seed)
        x = -0.0002928 + 1 * jax.random.normal(jax.random.fold_in(_rk, 1), (16, 64, 256), jnp.float32)
        _lenS = 64 - jax.random.randint(jax.random.fold_in(_rk, 7), (16,), 0, max(1, 64 // 4) + 1, jnp.int32)
        _lenS2 = 64 - jax.random.randint(jax.random.fold_in(_rk, 8), (16,), 0, max(1, 64 // 4) + 1, jnp.int32)
        _ctx_512P = jax.random.normal(jax.random.fold_in(_rk, 11), (16, 16, 64), jnp.float32)
        _ctx_512c = jax.random.dirichlet(jax.random.fold_in(_rk, 511), 0.3 * jnp.ones((16,), jnp.float32), (16, 64))
        _ctx_512t = jnp.einsum('bsk,bkd->bsd', _ctx_512c, _ctx_512P)
        _ctx_512t = _ctx_512t * jax.lax.rsqrt(jnp.mean(jnp.square(_ctx_512t)) + 1e-12) * 0.953939
        ctx_512 = 0.000227908 + 0.99994 * (_ctx_512t + 0.3 * jax.random.normal(jax.random.fold_in(_rk, 611), (16, 64, 64), jnp.float32))
        _g = jax.random.normal(jax.random.fold_in(_rk, 9001), (2, 2), jnp.float32)
        _g = jnp.sign(_g) * jnp.maximum(jnp.abs(_g), 1.0) + (_g == 0) * 1.0
        g_xattn = _g[0]
        g_ffn = _g[1]
        return (x, ctx_512, g_xattn, g_ffn)
    x, ctx_512, g_xattn, g_ffn = _rec_inputs()

    def _L0_xattn_setup():
        import jax, jax.numpy as jnp
        import numpy as np
        B, S, L = (2, 128, 128)
        DIM_Q, H, K, D_C, D_CQ, R = (256, 16, 128, 64, 192, 64)

        def _rope_tables(length, dim):
            inv = 1.0 / 10000.0 ** (jnp.arange(0, dim, 2, dtype=jnp.float32) / dim)
            f = jnp.arange(length, dtype=jnp.float32)[:, None] * inv[None, :]
            sin = jnp.repeat(jnp.sin(f), 2, axis=-1)
            cos = jnp.repeat(jnp.cos(f), 2, axis=-1)
            return (sin, cos)

        def _rotate_half(x):
            half = x.shape[-1] // 2
            return jnp.concatenate([-x[..., half:], x[..., :half]], axis=-1)

        def _apply_rope(x, sin, cos):
            return x * cos + _rotate_half(x) * sin
        key = jax.random.key(seed)
        ks = jax.random.split(key, 8)
        return {'hidden_q': jax.random.normal(ks[0], (B, S, DIM_Q), jnp.float32), 'kv_c': jax.random.normal(ks[1], (B, L, D_C), jnp.float32), 'Wq': jax.random.normal(ks[2], (H * K, DIM_Q), jnp.float32) / np.sqrt(DIM_Q).astype(np.float32), 'w_kc_q': jax.random.normal(ks[3], (H, K, D_CQ), jnp.float32) / np.sqrt(K).astype(np.float32), 'w_kc_kv': jax.random.normal(ks[4], (H, K, D_C), jnp.float32) / np.sqrt(K).astype(np.float32), 'W_qr': jax.random.normal(ks[5], (H, D_CQ, R), jnp.float32) / np.float32(np.sqrt(D_CQ) * np.sqrt(R)), 'W_kr': jax.random.normal(ks[6], (H, D_C, R), jnp.float32) / np.sqrt(D_C).astype(np.float32), 'Wo': jax.random.normal(ks[7], (DIM_Q, H * K), jnp.float32) / np.sqrt(H * K).astype(np.float32)}
    _L0_xattn_all = _L0_xattn_setup()
    _L0_xattn_in = {k: v for k, v in _L0_xattn_all.items() if k in ('Wq', 'w_kc_q', 'w_kc_kv', 'W_qr', 'W_kr', 'Wo')}
    del _L0_xattn_all

    def _L0_ffn_setup():
        import jax, jax.numpy as jnp
        import numpy as np
        NUM_EXPERTS = 8
        TOP_K = 2
        MODEL_DIM = 256
        INTER_DIM = 128
        GATE_SCALE = 1.0
        UP_SCALE = 0.0
        key = jax.random.key(seed)
        k1, k2, k3, k4 = jax.random.split(key, 4)
        hidden_states = jax.random.normal(k1, (2, 256, MODEL_DIM), jnp.float32)
        router_gate = jax.random.normal(k2, (NUM_EXPERTS, MODEL_DIM), jnp.float32) * 0.02
        expert_gate_up = jax.random.normal(k3, (NUM_EXPERTS, MODEL_DIM, 2 * INTER_DIM), jnp.float32) * 0.02
        expert_down = jax.random.normal(k4, (NUM_EXPERTS, INTER_DIM, MODEL_DIM), jnp.float32) * 0.02
        return {'hidden_states': hidden_states, 'router_gate': router_gate, 'expert_gate_up': expert_gate_up, 'expert_down': expert_down}
    _L0_ffn_all = _L0_ffn_setup()
    _L0_ffn_in = {k: v for k, v in _L0_ffn_all.items() if k in ('router_gate', 'expert_gate_up', 'expert_down')}
    del _L0_ffn_all

    def _L1_xattn_setup():
        import jax, jax.numpy as jnp
        import numpy as np
        B, S, L = (2, 128, 128)
        DIM_Q, H, K, D_C, D_CQ, R = (256, 16, 128, 64, 192, 64)

        def _rope_tables(seq_len, dim, dtype):
            inv_freq = 1.0 / 10000.0 ** (jnp.arange(0, dim, 2, dtype=dtype) / dim)
            t = jnp.arange(seq_len, dtype=dtype)
            freqs = t[:, None] * inv_freq[None, :]
            sin = jnp.repeat(jnp.sin(freqs), 2, axis=-1)
            cos = jnp.repeat(jnp.cos(freqs), 2, axis=-1)
            return (sin, cos)

        def _rotate_half(x):
            h = x.shape[-1] // 2
            return jnp.concatenate([-x[..., h:], x[..., :h]], axis=-1)
        key = jax.random.key(seed)
        ks = jax.random.split(key, 8)
        s_in = 1.0 / np.sqrt(DIM_Q)
        s_k = 1.0 / np.sqrt(K)
        s_cq = 1.0 / np.sqrt(D_CQ)
        s_c = 1.0 / np.sqrt(D_C)
        return {'hidden_q': jax.random.normal(ks[0], (B, S, DIM_Q), jnp.float32), 'kv_c': jax.random.normal(ks[1], (B, L, D_C), jnp.float32), 'Wq': jax.random.normal(ks[2], (H * K, DIM_Q), jnp.float32) * s_in, 'w_kc_q': jax.random.normal(ks[3], (H, K, D_CQ), jnp.float32) * s_k, 'w_kc_kv': jax.random.normal(ks[4], (H, K, D_C), jnp.float32) * s_k, 'W_qr': jax.random.normal(ks[5], (H, D_CQ, R), jnp.float32) * s_cq / np.sqrt(R), 'W_kr': jax.random.normal(ks[6], (H, D_C, R), jnp.float32) * s_c, 'Wo': jax.random.normal(ks[7], (DIM_Q, H * K), jnp.float32) * s_k}
    _L1_xattn_all = _L1_xattn_setup()
    _L1_xattn_in = {k: v for k, v in _L1_xattn_all.items() if k in ('Wq', 'w_kc_q', 'w_kc_kv', 'W_qr', 'W_kr', 'Wo')}
    del _L1_xattn_all

    def _L1_ffn_setup():
        import jax, jax.numpy as jnp
        import numpy as np
        TOPK = 2
        NORM_TOPK = True
        SCALE = 1.0
        EPS = 1e-09
        key = jax.random.key(seed)
        ks = jax.random.split(key, 9)
        h, i, E = (256, 128, 16)
        std = 0.02
        return {'x': jax.random.normal(ks[0], (1, 256, h), jnp.float32), 'Wr': jax.random.normal(ks[1], (E, h), jnp.float32) * std, 'bias': jnp.zeros((E,), jnp.float32), 'Wg': jax.random.normal(ks[2], (E, h, i), jnp.float32) * std, 'Wu': jax.random.normal(ks[3], (E, h, i), jnp.float32) * std, 'Wd': jax.random.normal(ks[4], (E, i, h), jnp.float32) * std, 'sWg': jax.random.normal(ks[5], (h, i), jnp.float32) * std, 'sWu': jax.random.normal(ks[6], (h, i), jnp.float32) * std, 'sWd': jax.random.normal(ks[7], (i, h), jnp.float32) * std}
    _L1_ffn_all = _L1_ffn_setup()
    _L1_ffn_in = {k: v for k, v in _L1_ffn_all.items() if k in ('Wr', 'bias', 'Wg', 'Wu', 'Wd', 'sWg', 'sWu', 'sWd')}
    del _L1_ffn_all
    return {'x': x, 'ctx_512': ctx_512, 'g_xattn': g_xattn, 'g_ffn': g_ffn, 'L0_xattn_Wq': _L0_xattn_in['Wq'], 'L0_xattn_w_kc_q': _L0_xattn_in['w_kc_q'], 'L0_xattn_w_kc_kv': _L0_xattn_in['w_kc_kv'], 'L0_xattn_W_qr': _L0_xattn_in['W_qr'], 'L0_xattn_W_kr': _L0_xattn_in['W_kr'], 'L0_xattn_Wo': _L0_xattn_in['Wo'], 'L0_ffn_router_gate': _L0_ffn_in['router_gate'], 'L0_ffn_expert_gate_up': _L0_ffn_in['expert_gate_up'], 'L0_ffn_expert_down': _L0_ffn_in['expert_down'], 'L1_xattn_Wq': _L1_xattn_in['Wq'], 'L1_xattn_w_kc_q': _L1_xattn_in['w_kc_q'], 'L1_xattn_w_kc_kv': _L1_xattn_in['w_kc_kv'], 'L1_xattn_W_qr': _L1_xattn_in['W_qr'], 'L1_xattn_W_kr': _L1_xattn_in['W_kr'], 'L1_xattn_Wo': _L1_xattn_in['Wo'], 'L1_ffn_Wr': _L1_ffn_in['Wr'], 'L1_ffn_bias': _L1_ffn_in['bias'], 'L1_ffn_Wg': _L1_ffn_in['Wg'], 'L1_ffn_Wu': _L1_ffn_in['Wu'], 'L1_ffn_Wd': _L1_ffn_in['Wd'], 'L1_ffn_sWg': _L1_ffn_in['sWg'], 'L1_ffn_sWu': _L1_ffn_in['sWu'], 'L1_ffn_sWd': _L1_ffn_in['sWd']}

def reference(x, ctx_512, g_xattn, g_ffn, L0_xattn_Wq, L0_xattn_w_kc_q, L0_xattn_w_kc_kv, L0_xattn_W_qr, L0_xattn_W_kr, L0_xattn_Wo, L0_ffn_router_gate, L0_ffn_expert_gate_up, L0_ffn_expert_down, L1_xattn_Wq, L1_xattn_w_kc_q, L1_xattn_w_kc_kv, L1_xattn_W_qr, L1_xattn_W_kr, L1_xattn_Wo, L1_ffn_Wr, L1_ffn_bias, L1_ffn_Wg, L1_ffn_Wu, L1_ffn_Wd, L1_ffn_sWg, L1_ffn_sWu, L1_ffn_sWd):
    import jax
    import jax.numpy as jnp

    def _L0_xattn_ref(hidden_q, kv_c, Wq, w_kc_q, w_kc_kv, W_qr, W_kr, Wo):
        import jax, jax.numpy as jnp
        import numpy as np
        B, S, L = (2, 128, 128)
        DIM_Q, H, K, D_C, D_CQ, R = (256, 16, 128, 64, 192, 64)

        def _rope_tables(length, dim):
            inv = 1.0 / 10000.0 ** (jnp.arange(0, dim, 2, dtype=jnp.float32) / dim)
            f = jnp.arange(length, dtype=jnp.float32)[:, None] * inv[None, :]
            sin = jnp.repeat(jnp.sin(f), 2, axis=-1)
            cos = jnp.repeat(jnp.cos(f), 2, axis=-1)
            return (sin, cos)

        def _rotate_half(x):
            half = x.shape[-1] // 2
            return jnp.concatenate([-x[..., half:], x[..., :half]], axis=-1)

        def _apply_rope(x, sin, cos):
            return x * cos + _rotate_half(x) * sin
        Bv, Sv, _ = hidden_q.shape
        _, Lv, _ = kv_c.shape
        q_hk = (hidden_q @ Wq.T).reshape(Bv, Sv, H, K)
        q_big = jnp.einsum('bshk,hkq->bshq', q_hk, w_kc_q)
        sin_q, cos_q = _rope_tables(Sv, D_CQ)
        q_big = _apply_rope(q_big, sin_q[None, :, None, :], cos_q[None, :, None, :])
        sin_k, cos_k = _rope_tables(Lv, D_C)
        kv_r = _apply_rope(kv_c, sin_k[None], cos_k[None])
        q_r = jnp.einsum('bshq,hqr->bhsr', q_big, W_qr)
        k_r = jnp.einsum('bld,hdr->bhlr', kv_r, W_kr)
        scores = jnp.einsum('bhsr,bhlr->bhsl', q_r, k_r)
        attn = jax.nn.softmax(scores, axis=-1)
        ctx_c = jnp.einsum('bhsl,bld->bhsd', attn, kv_r)
        ctx_lat = jnp.einsum('bhsd,hkd->bhsk', ctx_c, w_kc_kv)
        ctx = ctx_lat.transpose(0, 2, 1, 3).reshape(Bv, Sv, H * K)
        return ctx @ Wo.T

    def _L0_ffn_ref(hidden_states, router_gate, expert_gate_up, expert_down):
        import jax, jax.numpy as jnp
        import numpy as np
        NUM_EXPERTS = 8
        TOP_K = 2
        MODEL_DIM = 256
        INTER_DIM = 128
        GATE_SCALE = 1.0
        UP_SCALE = 0.0
        orig_shape = hidden_states.shape
        hs = hidden_states.reshape(-1, orig_shape[-1])
        T = hs.shape[0]
        logits = hs @ router_gate.T
        probs = jax.nn.softmax(logits.astype(jnp.float32), axis=-1)
        topk_scores, topk_idx = jax.lax.top_k(probs, TOP_K)
        topk_scores = topk_scores / jnp.sum(topk_scores, axis=-1, keepdims=True)
        scores_f = topk_scores.T.reshape(-1).astype(hs.dtype)
        ids_f = topk_idx.T.reshape(-1)
        order = jnp.argsort(ids_f)
        sorted_ids = ids_f[order]
        scores_sorted = scores_f[order]
        token_slots = order % T
        x = hs[token_slots]
        inter = jnp.zeros((x.shape[0], 2 * INTER_DIM), x.dtype)
        for e in range(NUM_EXPERTS):
            m = (sorted_ids == e)[:, None]
            inter = inter + jnp.where(m, x, 0) @ expert_gate_up[e]
        gate = inter[..., 0::2]
        up = inter[..., 1::2]
        h = (up + UP_SCALE) * jax.nn.silu(gate * GATE_SCALE)
        out_rows = jnp.zeros((x.shape[0], MODEL_DIM), x.dtype)
        for e in range(NUM_EXPERTS):
            m = (sorted_ids == e)[:, None]
            out_rows = out_rows + jnp.where(m, h, 0) @ expert_down[e]
        out = jnp.zeros_like(hs).at[token_slots].add(out_rows * scores_sorted[:, None])
        return out.reshape(orig_shape)

    def _L1_xattn_ref(hidden_q, kv_c, Wq, w_kc_q, w_kc_kv, W_qr, W_kr, Wo):
        import jax, jax.numpy as jnp
        import numpy as np
        B, S, L = (2, 128, 128)
        DIM_Q, H, K, D_C, D_CQ, R = (256, 16, 128, 64, 192, 64)

        def _rope_tables(seq_len, dim, dtype):
            inv_freq = 1.0 / 10000.0 ** (jnp.arange(0, dim, 2, dtype=dtype) / dim)
            t = jnp.arange(seq_len, dtype=dtype)
            freqs = t[:, None] * inv_freq[None, :]
            sin = jnp.repeat(jnp.sin(freqs), 2, axis=-1)
            cos = jnp.repeat(jnp.cos(freqs), 2, axis=-1)
            return (sin, cos)

        def _rotate_half(x):
            h = x.shape[-1] // 2
            return jnp.concatenate([-x[..., h:], x[..., :h]], axis=-1)
        b, s, _ = hidden_q.shape
        l = kv_c.shape[1]
        q_hk = (hidden_q @ Wq.T).reshape(b, s, H, K)
        q_big = jnp.einsum('bshk,hkq->bshq', q_hk, w_kc_q)
        sin, cos = _rope_tables(l, D_C, kv_c.dtype)
        kv_rope = kv_c * cos[None] + _rotate_half(kv_c) * sin[None]
        q_r = jnp.einsum('bshq,hqr->bhsr', q_big, W_qr)
        k_r = jnp.einsum('bld,hdr->bhlr', kv_rope, W_kr)
        scores = jnp.einsum('bhsr,bhlr->bhsl', q_r, k_r)
        attn = jax.nn.softmax(scores, axis=-1)
        ctx_c = jnp.einsum('bhsl,bld->bhsd', attn, kv_rope)
        ctx_lat = jnp.einsum('bhsd,hkd->bshk', ctx_c, w_kc_kv)
        out = ctx_lat.reshape(b, s, H * K) @ Wo.T
        return out

    def _L1_ffn_ref(x, Wr, bias, Wg, Wu, Wd, sWg, sWu, sWd):
        import jax, jax.numpy as jnp
        import numpy as np
        TOPK = 2
        NORM_TOPK = True
        SCALE = 1.0
        EPS = 1e-09
        b, s, h = x.shape
        E = Wr.shape[0]
        xt = x.reshape(b * s, h)
        logits = xt @ Wr.T + bias
        probs = jax.nn.softmax(logits, axis=-1)
        topk_val, topk_idx = jax.lax.top_k(probs, TOPK)
        if NORM_TOPK:
            w = topk_val / (jnp.sum(topk_val, axis=-1, keepdims=True) + EPS)
        else:
            w = topk_val
        w = w * SCALE
        g = jnp.einsum('th,ehi->tei', xt, Wg)
        u = jnp.einsum('th,ehi->tei', xt, Wu)
        y = jnp.einsum('tei,eih->teh', jax.nn.silu(g) * u, Wd)
        oh = jax.nn.one_hot(topk_idx, E, dtype=x.dtype)
        routed = jnp.einsum('tke,tk,teh->th', oh, w, y)
        shared = jax.nn.silu(xt @ sWg) * (xt @ sWu) @ sWd
        return (routed + shared).reshape(b, s, h)
    x = x + jnp.tanh(g_xattn[0]) * _L0_xattn_ref(_layernorm(x, axis=-1), ctx_512, L0_xattn_Wq, L0_xattn_w_kc_q, L0_xattn_w_kc_kv, L0_xattn_W_qr, L0_xattn_W_kr, L0_xattn_Wo)
    x = x + jnp.tanh(g_ffn[0]) * _L0_ffn_ref(_layernorm(x, axis=-1), L0_ffn_router_gate, L0_ffn_expert_gate_up, L0_ffn_expert_down)
    x = x + jnp.tanh(g_xattn[1]) * _L1_xattn_ref(_layernorm(x, axis=-1), ctx_512, L1_xattn_Wq, L1_xattn_w_kc_q, L1_xattn_w_kc_kv, L1_xattn_W_qr, L1_xattn_W_kr, L1_xattn_Wo)
    x = x + jnp.tanh(g_ffn[1]) * _L1_ffn_ref(_layernorm(x, axis=-1), L1_ffn_Wr, L1_ffn_bias, L1_ffn_Wg, L1_ffn_Wu, L1_ffn_Wd, L1_ffn_sWg, L1_ffn_sWu, L1_ffn_sWd)
    return x

_drawn_inputs = setup_inputs


def setup_inputs(seed=0):
    import zlib

    import numpy as np

    out = dict(_drawn_inputs(seed))
    spreads = {'g_ffn': (-1.0, 0.6), 'L1_ffn_bias': (0.0, 0.8)}
    factors = {'L0_ffn_router_gate': 8.0,
     'L0_ffn_expert_gate_up': 8.0,
     'L0_ffn_expert_down': 8.0,
     'L1_ffn_Wr': 8.0,
     'L1_ffn_Wg': 8.0,
     'L1_ffn_Wu': 8.0,
     'L1_ffn_Wd': 8.0,
     'L1_ffn_sWg': 8.0,
     'L1_ffn_sWu': 8.0,
     'L1_ffn_sWd': 8.0}
    for name, (base, spread) in spreads.items():
        noise = np.random.default_rng([zlib.crc32(name.encode()), seed]).standard_normal(out[name].shape)
        drawn = base * np.exp(spread * noise) if base else spread * noise
        out[name] = jnp.asarray(drawn.astype(out[name].dtype))
    for name, factor in factors.items():
        out[name] = (out[name] * factor).astype(out[name].dtype)
    return out
```

```python
from contextlib import ExitStack

import numpy as np

import concourse.bass as bass
from concourse import mybir

P = 128
NB, S, DM = 16, 64, 256
L, DC = 64, 64
H, K, DQ, R = 16, 128, 192, 64
HP = H // 2
TOK = NB * S
NT = TOK // P
NCH = DM // P
HALF = 512
E0, E1 = 8, 16
INTER = 128
EPS_LN, EPS_TOPK = 1e-5, 1e-9
RSQRT_GUESS = 0x5F3759DF
BIG = 4.0

F32 = mybir.dt.float32
I32 = mybir.dt.int32
ALU = mybir.AluOpType
ACT = mybir.ActivationFunctionType
AX = mybir.AxisListType.X

WQ0, WCQ0, WRA, WRC, WRBC, WRBS, WKR0, WO0, WCK0 = 0, 512, 896, 1024, 1152, 1280, 1408, 1536, 2048
PACK0 = 2176
WQ1, WCQ1, WQR1, WKR1, WO1, WCK1 = 0, 512, 1024, 1280, 1408, 1920
PACK1 = 2048
PACKF = 4 * INTER + DM
QH = DQ // 2


def build(nc, x, kvT, kvTrot, kv, cosT, sinT, cosR, sinR, cosQ, sinQ, attn0, attn1, ffn0, ffn1,
          router0, router1, bias1, gates, ident_d, iota_d, out):
    with ExitStack() as ctx:
        def sb(name, shape):
            return ctx.enter_context(nc.sbuf_tensor(name, shape, F32))

        def sem(name):
            return ctx.enter_context(nc.semaphore(name))

        X = sb("X", [P, NT, DM])
        xn = sb("xn", [P, NT, DM])
        xnT = sb("xnT", [P, NCH, TOK])
        ident = sb("ident", [P, P])
        kvrT = sb("kvrT", [P, TOK])
        kbd = sb("kbd", [P, NB, 2 * L])
        vbd = sb("vbd", [P, NB, 2 * DC])
        cosT_s, sinT_s = sb("cosT_s", [P, L]), sb("sinT_s", [P, L])
        cosR_s, sinR_s = sb("cosR_s", [P, DC]), sb("sinR_s", [P, DC])
        cosQ_s, sinQ_s = sb("cosQ_s", [P, 3, S]), sb("sinQ_s", [P, 3, S])
        W = [sb(f"W{u}", [P, PACK0]) for u in range(2)]
        A_sb = sb("A_sb", [P, NCH, 2 * DQ])
        qc = sb("qc", [P, 3, TOK])
        qs = sb("qs", [P, 3, TOK])
        qrT = sb("qrT", [P, TOK])
        probs = sb("probs", [P, NT, 2, L])
        rowmax = sb("rowmax", [P, NT, 2])
        rowsum = sb("rowsum", [P, NT, 2])
        rowrec = sb("rowrec", [P, NT, 2])
        PT = sb("PT", [P, HP, TOK])
        N_sb = sb("N_sb", [P, HP, DM])
        T1_sb = sb("T1_sb", [P, 2 * R])
        M_sb = sb("M_sb", [P, NCH, 2 * R])
        WF = [sb(f"WF{u}", [P, PACKF]) for u in range(2)]
        silu = sb("silu", [P, 2, HALF])
        hT = [sb(f"hT{u}", [P, TOK]) for u in range(2)]
        ropeA, ropeB = hT[0], hT[1]
        kvT_s, kvTrot_s, kv_s = qc[:, 0, :], qc[:, 1, :], qc[:, 2, :]
        stats = sb("stats", [P, NT, 6])
        meanvar = sb("meanvar", [P, NT, 2])
        rstd, varep, newton = sb("rstd", [P, NT]), sb("varep", [P, NT]), sb("newton", [P, NT])
        gate = sb("gate", [P, 4])
        tgate = sb("tgate", [P, 4])
        wr = [sb("wr0", [P, NCH, E0]), sb("wr1", [P, NCH, E1])]
        bias_s = sb("bias_s", [P, E1])
        iota = sb("iota", [P, E1])
        coef = sb("coef", [P, NT, E1 + 1])
        rt = [sb(f"rt{n}", [P, NT, E1]) for n in range(4)]
        rs = [sb(f"rs{n}", [P, NT]) for n in range(6)]
        psum = [ctx.enter_context(nc.psum_tensor(f"ps{n}", [P, HALF], F32)) for n in range(8)]

        x_loaded = [sem(f"x_loaded{k}") for k in range(2)]
        const_loaded, kv_loaded = sem("const_loaded"), sem("kv_loaded")
        gate_ready, zeros_ready = sem("gate_ready"), sem("zeros_ready")
        kv_step, kv_ready = sem("kv_step"), sem("kv_ready")
        out_written = sem("out_written")

        block = ctx.enter_context(nc.Block())

        class LnSems:
            def __init__(s, n):
                s.stat = sem(f"ln{n}_stat")
                s.agg = sem(f"ln{n}_agg")
                s.rstd = sem(f"ln{n}_rstd")
                s.xn = sem(f"ln{n}_xn")
                s.tp = sem(f"ln{n}_tp")
                s.xnT = sem(f"ln{n}_xnT")

        class AttnSems:
            def __init__(s, n):
                p = f"at{n}_"
                s.w = [sem(f"{p}w{u}") for u in range(2)]
                s.a, s.a_ev = sem(p + "a"), sem(p + "a_ev")
                s.m, s.m_ev = sem(p + "m"), sem(p + "m_ev")
                s.n, s.n_ev = sem(p + "n"), sem(p + "n_ev")
                s.q, s.q_ev = sem(p + "q"), sem(p + "q_ev")
                s.kr, s.kbd = sem(p + "kr"), sem(p + "kbd")
                s.qr, s.qr_ev = sem(p + "qr"), sem(p + "qr_ev")
                s.s = sem(p + "s")
                s.max, s.sub = sem(p + "max"), sem(p + "sub")
                s.exp, s.sum = sem(p + "exp"), sem(p + "sum")
                s.rec, s.p = sem(p + "rec"), sem(p + "p")
                s.t, s.t_ev = sem(p + "t"), sem(p + "t_ev")
                s.c, s.c_ev = sem(p + "c"), sem(p + "c_ev")
                s.o, s.x = sem(p + "o"), sem(p + "x")

        class FfnSems:
            def __init__(s, n):
                p = f"ff{n}_"
                s.w = [sem(f"{p}w{u}") for u in range(2)]
                s.logits, s.route = sem(p + "logits"), sem(p + "route")
                s.gu, s.silu, s.h = sem(p + "gu"), sem(p + "silu"), sem(p + "h")
                s.d, s.x = sem(p + "d"), sem(p + "x")

        ln = [LnSems(n) for n in range(4)]
        at = [AttnSems(n) for n in range(2)]
        ff = [FfnSems(n) for n in range(2)]
        EXPERTS = [E0, E1 + 1]

        @block.sync
        def _(sp):
            xv = x.rearrange("(t p) d -> p t d", p=P)
            sp.dma_start(X[:, 0:4, :], xv[:, 0:4, :]).then_inc(x_loaded[0], 16)
            sp.dma_start(X[:, 4:8, :], xv[:, 4:8, :]).then_inc(x_loaded[1], 16)
            sp.dma_start(W[0][:, 0:PACK0], attn0[0]).then_inc(at[0].w[0], 16)
            for dst, src in ((ident[:], ident_d), (cosQ_s[:], cosQ), (sinQ_s[:], sinQ),
                             (gate[:], gates), (bias_s[:], bias1), (iota[:], iota_d),
                             (wr[0][:], router0), (wr[1][:], router1)):
                sp.dma_start(dst, src).then_inc(const_loaded, 16)
            for dst, src in ((kvT_s, kvT), (kvTrot_s, kvTrot), (kv_s, kv), (cosT_s[:], cosT),
                             (sinT_s[:], sinT), (cosR_s[:], cosR), (sinR_s[:], sinR)):
                sp.dma_start(dst, src).then_inc(kv_loaded, 16)
            sp.dma_start(W[1][:, 0:PACK0], attn0[1]).then_inc(at[0].w[1], 16)
            for n, (packs, cols) in enumerate(((attn0, PACK0), (attn1, PACK1))):
                fpack = (ffn0, ffn1)[n]
                for u in range(2):
                    if n:
                        sp.wait_ge(ff[0].d, NT // 2 * (EXPERTS[0] - 1 + u))
                    sp.dma_start(WF[u][:], fpack[u]).then_inc(ff[n].w[u], 16)
                if n:
                    for u in range(2):
                        sp.wait_ge(at[0].qr, 2 * (HP - 1 + u))
                        sp.dma_start(W[u][:, 0:cols], packs[u]).then_inc(at[n].w[u], 16)
                with sp.Fori(0, HP // 2 - 1) as j:
                    for u in range(2):
                        if n:
                            sp.wait_ge(at[n].n, 2 * j + u + 1)
                        else:
                            sp.wait_ge(at[n].qr, 4 * j + 2 * u + 2)
                        sp.dma_start(W[u][:, 0:cols], packs[bass.ds(2 * j + 2 + u, 1)].rearrange("a p c -> (a p) c"))\
                            .then_inc(at[n].w[u], 16)
                if EXPERTS[n] > 3:
                    with sp.Fori(0, (EXPERTS[n] - 2) // 2) as j:
                        for u in range(2):
                            sp.wait_ge(ff[n].d, NT // 2 * (2 * j + u + 1))
                            sp.dma_start(WF[u][:], fpack[bass.ds(2 * j + 2 + u, 1)].rearrange("a p c -> (a p) c"))\
                                .then_inc(ff[n].w[u], 16)
                if EXPERTS[n] % 2:
                    sp.wait_ge(ff[n].d, NT // 2 * (EXPERTS[n] - 2))
                    sp.dma_start(WF[0][:], fpack[EXPERTS[n] - 1]).then_inc(ff[n].w[0], 16)
            ov = out.rearrange("(t p) d -> p t d", p=P)
            for t in range(NT):
                sp.wait_ge(ff[1].x, NT * (EXPERTS[1] - 1) + t + 1)
                sp.dma_start(ov[:, t, :], X[:, t, :]).then_inc(out_written, 16)
            sp.wait_ge(out_written, 16 * NT)

        @block.gpsimd
        def _(pool):
            nc.gpsimd.memset(vbd[:], 0.0).then_inc(zeros_ready, 1)
            nc.gpsimd.memset(kbd[:], 0.0).then_inc(zeros_ready, 1)
            nc.gpsimd.memset(coef[:], 1.0).then_inc(zeros_ready, 1)
            for n in range(2):
                with pool.Fori(0, HP) as i:
                    for h in range(2):
                        pool.wait_ge(at[n].rec, 2 * i + h + 1)
                        part = probs[:, 4 * h:4 * h + 4]
                        nc.gpsimd.tensor_tensor(
                            part, part, rowrec[:, 4 * h:4 * h + 4, :].unsqueeze(3).to_broadcast([P, 4, 2, L]),
                            ALU.mult).then_inc(at[n].p, 1)

        @block.tensor
        def _(pe):
            def layer_norm(n):
                for g in range(NT // 2):
                    for k in range(2):
                        t = 2 * g + k
                        pe.wait_ge(ln[n].xn, t + 1)
                        for c in range(NCH):
                            last = nc.tensor.transpose(psum[g][:, (2 * c + k) * P:(2 * c + k + 1) * P],
                                                       xn[:, t, c * P:(c + 1) * P], ident[:])
                    last.then_inc(ln[n].tp, 1)

            def scores(s, i):
                for h in range(2):
                    pe.wait_ge(s.kbd, 2 * i + h + 1)
                    pe.wait_ge(s.qr_ev, 2 * i + h + 1)
                    for t in range(4):
                        for b in range(2):
                            tok = (4 * h + t) * P + b * S
                            last = nc.tensor.matmul(psum[6 + h][b * S:(b + 1) * S, t * P:(t + 1) * P],
                                                    qrT[:, tok:tok + S], kbd[:, 2 * (4 * h + t) + b, :],
                                                    start=True, stop=True)
                    last.then_inc(s.s, 1)

            def transposes(s, i, banks):
                for h in range(2):
                    pe.wait_ge(s.p, 2 * i + h + 1)
                    for t in range(4):
                        last = nc.tensor.transpose(psum[banks[h]][:, t * P:(t + 1) * P],
                                                   probs[:, 4 * h + t].rearrange("p a l -> p (a l)"), ident[:])
                    last.then_inc(s.t, 1)

            def out_weights(s, w, bank, wo, wck):
                for a in range(2):
                    last = nc.tensor.matmul(psum[bank][a * DC:(a + 1) * DC, 0:DM],
                                            w[:, wck + a * DC:wck + (a + 1) * DC],
                                            w[:, wo + a * DM:wo + (a + 1) * DM], start=True, stop=True)
                last.then_inc(s.n, 1)

            def keys(s, w, h, bank, wkr):
                nc.tensor.matmul(psum[bank][:, :], w[:, wkr:wkr + 2 * R], kvrT[:, h * HALF:(h + 1) * HALF],
                                 start=True, stop=True).then_inc(s.kr, 1)

            def context_and_output(s):
                pe.wait_ge(s.t_ev, 2 * HP)
                for b in range(NB):
                    if b >= 8:
                        pe.wait_ge(s.c_ev, b - 7)
                    nc.tensor.matmul(psum[b % 8][:, :], vbd[:, b, :], PT[:, :, b * S:(b + 1) * S],
                                     start=True, stop=True).then_inc(s.c, 1)
                pe.wait_ge(s.n_ev, HP)
                for t in range(NT):
                    pe.wait_ge(s.c_ev, max(2 * t + 2, t + 9))
                    for p in range(HP):
                        last = nc.tensor.matmul(psum[t][:, 0:DM], PT[:, p, t * P:(t + 1) * P], N_sb[:, p, :],
                                                start=(p == 0), stop=(p == HP - 1))
                    last.then_inc(s.o, 1)

            def attention0():
                s = at[0]

                def query_weights(w):
                    for c in range(NCH):
                        for a in range(2):
                            last = nc.tensor.matmul(psum[c][:, a * DQ:(a + 1) * DQ],
                                                    w[:, WQ0 + a * DM + c * P:WQ0 + a * DM + (c + 1) * P],
                                                    w[:, WCQ0 + a * DQ:WCQ0 + (a + 1) * DQ], start=True, stop=True)
                        last.then_inc(s.a, 1)

                def body(i, u, count, first=False, final=False):
                    w = W[u]
                    pe.wait_ge(s.a_ev, 2 * i + 2)
                    for h in range(2):
                        for j in range(3):
                            n = 3 * h + j
                            if n == 2 and not first:
                                pe.wait_ge(s.kbd, 2 * i)
                            if n == 4 and not first:
                                pe.wait_ge(s.qr_ev, 2 * i)
                            for c in range(NCH):
                                last = nc.tensor.matmul(psum[n][:, :], A_sb[:, c, j * P:(j + 1) * P],
                                                        xnT[:, c, h * HALF:(h + 1) * HALF],
                                                        start=(c == 0), stop=(c == NCH - 1))
                            last.then_inc(s.q, 1)
                    if not first:
                        transposes(s, i - 1, (6, 7))
                    if not final:
                        pe.wait_ge(s.q_ev, 6 * i + 2)
                        pe.wait_ge(s.w[1 - u], 16 * (count + u))
                        query_weights(W[1 - u])
                    pe.wait_ge(s.q_ev, 6 * i + 3)
                    out_weights(s, w, 2, WO0, WCK0)
                    if first:
                        pe.wait_ge(kv_ready, 2)
                    pe.wait_ge(s.q_ev, 6 * i + 4)
                    keys(s, w, 0, 3, WKR0)
                    pe.wait_ge(s.n_ev, i + 1)
                    keys(s, w, 1, 2, WKR0)
                    for h in range(2):
                        pe.wait_ge(s.q_ev, 6 * i + 5 + h)
                        tk = slice(h * HALF, (h + 1) * HALF)
                        o = psum[4 + h]
                        steps = [(o[:, :], WRBC, 2 * R, qc[:, 2, tk]), (o[:, :], WRBS, 2 * R, qs[:, 2, tk])]
                        steps += [(o[a * R:(a + 1) * R, :], WRA + a * R, R, qc[:, a, tk]) for a in range(2)]
                        steps += [(o[a * R:(a + 1) * R, :], WRC + a * R, R, qs[:, a, tk]) for a in range(2)]
                        for k, (dst, col, m, rhs) in enumerate(steps):
                            last = nc.tensor.matmul(dst, w[:, col:col + m], rhs, start=(k == 0),
                                                    stop=(k >= len(steps) - 2), skip_group_check=True)
                        last.then_inc(s.qr, 1)
                    last_q = nc.tensor
                    if not first:
                        pe.wait_ge(s.t_ev, 2 * i)
                    scores(s, i)

                pe.wait_ge(s.w[0], 16)
                query_weights(W[0])
                body(0, 0, 1, first=True)
                with pe.Fori(0, HP // 2 - 1) as j:
                    body(2 * j + 1, 1, j + 1)
                    body(2 * j + 2, 0, j + 2)
                body(HP - 1, 1, HP // 2, final=True)
                transposes(s, HP - 1, (6, 7))
                context_and_output(s)

            def attention1():
                s = at[1]

                def t1(w):
                    for a in range(2):
                        for c in range(2):
                            last = nc.tensor.matmul(psum[2][:, a * R:(a + 1) * R],
                                                    w[0:QH, WCQ1 + (2 * a + c) * K:WCQ1 + (2 * a + c + 1) * K],
                                                    w[0:QH, WQR1 + (2 * a + c) * R:WQR1 + (2 * a + c + 1) * R],
                                                    start=(c == 0), stop=(c == 1))
                    last.then_inc(s.a, 1)

                def m(w):
                    for c in range(NCH):
                        for a in range(2):
                            last = nc.tensor.matmul(psum[4][:, (2 * c + a) * R:(2 * c + a + 1) * R],
                                                    w[:, WQ1 + a * DM + c * P:WQ1 + a * DM + (c + 1) * P],
                                                    T1_sb[:, a * R:(a + 1) * R], start=True, stop=True)
                    last.then_inc(s.m, 1)

                def body(i, u, count, first=False, final=False):
                    w = W[u]
                    if not first:
                        pe.wait_ge(s.a_ev, i + 1)
                        pe.wait_ge(s.n_ev, i)
                    keys(s, w, 0, 2, WKR1)
                    keys(s, w, 1, 3, WKR1)
                    pe.wait_ge(s.m_ev, i + 1)
                    if not first:
                        pe.wait_ge(s.qr_ev, 2 * i)
                    for h in range(2):
                        for c in range(NCH):
                            last = nc.tensor.matmul(psum[4 + h][:, :], M_sb[:, c, :],
                                                    xnT[:, c, h * HALF:(h + 1) * HALF],
                                                    start=(c == 0), stop=(c == NCH - 1))
                        last.then_inc(s.qr, 1)
                    if not first:
                        transposes(s, i - 1, (0, 1))
                    pe.wait_ge(s.kbd, 2 * i + 2)
                    if not final:
                        pe.wait_ge(s.w[1 - u], 16 * (count + u))
                        t1(W[1 - u])
                    out_weights(s, w, 3, WO1, WCK1)
                    scores(s, i)
                    if not final:
                        pe.wait_ge(s.a_ev, i + 2)
                        m(W[1 - u])
                    if not first:
                        pe.wait_ge(s.t_ev, 2 * i)

                pe.wait_ge(s.w[0], 16)
                t1(W[0])
                pe.wait_ge(s.a_ev, 1)
                m(W[0])
                body(0, 0, 1, first=True)
                with pe.Fori(0, HP // 2 - 1) as j:
                    body(2 * j + 1, 1, j + 1)
                    body(2 * j + 2, 0, j + 2)
                body(HP - 1, 1, HP // 2, final=True)
                transposes(s, HP - 1, (0, 1))
                context_and_output(s)

            def experts(n):
                s, ne = ff[n], EXPERTS[n]
                nr = (E0, E1)[n]
                for t in range(NT):
                    for c in range(NCH):
                        last = nc.tensor.matmul(psum[7][:, t * nr:(t + 1) * nr], xnT[:, c, t * P:(t + 1) * P],
                                                wr[n][:, c, :], start=(c == 0), stop=(c == NCH - 1))
                last.then_inc(s.logits, 1)

                def gate_up(i, u, count, first=False):
                    pe.wait_ge(s.w[u], 16 * count)
                    for h in range(2):
                        if not first:
                            pe.wait_ge(s.h, 2 * i + h - 1)
                        for k in range(2):
                            for c in range(NCH):
                                col = (2 * k + c) * INTER
                                last = nc.tensor.matmul(psum[2 * h + k][:, :], WF[u][:, col:col + INTER],
                                                        xnT[:, c, h * HALF:(h + 1) * HALF],
                                                        start=(c == 0), stop=(c == NCH - 1))
                            last.then_inc(s.gu, 1)

                def down(i, u, first=False):
                    for t in range(NT):
                        if t % 4 == 0:
                            pe.wait_ge(s.h, 2 * i + t // 4 + 1)
                        if t % 2 == 0 and not first:
                            pe.wait_ge(s.x, NT * (i - 1) + t + 2)
                        last = nc.tensor.matmul(psum[4 + t // 2][:, (t % 2) * DM:(t % 2 + 1) * DM],
                                                hT[u][:, t * P:(t + 1) * P], WF[u][:, 4 * INTER:4 * INTER + DM],
                                                start=True, stop=True)
                        if t % 2:
                            last.then_inc(s.d, 1)

                gate_up(0, 0, 1, first=True)
                pe.wait_ge(s.route, 1)
                gate_up(1, 1, 1)
                down(0, 0, first=True)
                pairs = (ne - 2) // 2
                with pe.Fori(0, pairs) as j:
                    gate_up(2 * j + 2, 0, j + 2)
                    down(2 * j + 1, 1)
                    gate_up(2 * j + 3, 1, j + 2)
                    down(2 * j + 2, 0)
                if ne % 2:
                    gate_up(ne - 1, 0, pairs + 2)
                    down(ne - 2, 1)
                    down(ne - 1, 0)
                else:
                    down(ne - 1, 1)

            pe.wait_ge(const_loaded, 16 * 8)
            layer_norm(0)
            pe.wait_ge(ln[0].xnT, NT // 2)
            attention0()
            pe.wait_ge(at[0].x, NT)
            layer_norm(1)
            pe.wait_ge(ln[1].xnT, NT // 2)
            experts(0)
            pe.wait_ge(ff[0].x, NT * EXPERTS[0])
            layer_norm(2)
            pe.wait_ge(ln[2].xnT, NT // 2)
            attention1()
            pe.wait_ge(at[1].x, NT)
            layer_norm(3)
            pe.wait_ge(ln[3].xnT, NT // 2)
            experts(1)

        @block.scalar
        def _(act):
            def copy(dst, src):
                return nc.scalar.activation(dst, src, ACT.Copy)

            def layer_norm(n):
                for g in range(NT // 2):
                    act.wait_ge(ln[n].tp, g + 1)
                    copy(xnT[:, :, 2 * g * P:(2 * g + 2) * P],
                         psum[g][:].rearrange("p (c k) -> p c k", c=NCH)).then_inc(ln[n].xnT, 1)

            def exps(s, i, h):
                act.wait_ge(s.sub, 2 * i + h + 1)
                part = probs[:, 4 * h:4 * h + 4]
                nc.scalar.activation(part, part, ACT.Exp).then_inc(s.exp, 1)

            def keys(s, i, h, bank):
                act.wait_ge(s.kr, 2 * i + h + 1)
                src = psum[bank][:].rearrange("p (b l) -> p b l", l=L)
                copy(kbd[0:R, 8 * h:8 * h + 8, 0:L], src[0:R])
                copy(kbd[R:P, 8 * h:8 * h + 8, L:2 * L], src[R:P]).then_inc(s.kbd, 1)

            def queries(s, i):
                for h in range(2):
                    act.wait_ge(s.qr, 2 * i + h + 1)
                    copy(qrT[:, h * HALF:(h + 1) * HALF], psum[4 + h][:]).then_inc(s.qr_ev, 1)

            def transposed(s, i, banks):
                for h in range(2):
                    act.wait_ge(s.t, 2 * i + h + 1)
                    copy(PT[:, bass.ds(i, 1), h * HALF:(h + 1) * HALF].rearrange("p a t -> p (a t)"),
                         psum[banks[h]][:]).then_inc(s.t_ev, 1)

            def out_weights(s, i, bank):
                act.wait_ge(s.n, i + 1)
                copy(N_sb[:, bass.ds(i, 1), :].rearrange("p a t -> p (a t)"), psum[bank][:, 0:DM]).then_inc(s.n_ev, 1)

            def context(s):
                for b in range(NB):
                    act.wait_ge(s.c, b + 1)
                    copy(PT[:, :, b * S:(b + 1) * S],
                         psum[b % 8][:].rearrange("p (h s) -> p h s", h=HP)).then_inc(s.c_ev, 1)

            def attention0():
                s = at[0]

                def query_weights(i):
                    for c in range(NCH):
                        act.wait_ge(s.a, 2 * i + c + 1)
                        src = psum[c][:, 0:2 * DQ].rearrange("p (a q) -> p a q", a=2)
                        copy(A_sb[:, c, 0:2 * P].rearrange("p (a q) -> p a q", a=2), src[:, :, 0:P])
                        copy(A_sb[:, c, 2 * P:2 * DQ].rearrange("p (a q) -> p a q", a=2), src[:, :, P:DQ])\
                            .then_inc(s.a_ev, 1)

                def body(i, first=False, final=False):
                    if not first:
                        exps(s, i - 1, 0)
                        exps(s, i - 1, 1)
                        transposed(s, i - 1, (6, 7))
                    if not final:
                        query_weights(i + 1)
                    out_weights(s, i, 2)
                    if first:
                        act.wait_ge(zeros_ready, 2)
                    keys(s, i, 0, 3)
                    keys(s, i, 1, 2)
                    queries(s, i)

                query_weights(0)
                body(0, first=True)
                with act.Fori(1, HP - 1) as i:
                    body(i)
                body(HP - 1, final=True)
                exps(s, HP - 1, 0)
                exps(s, HP - 1, 1)
                transposed(s, HP - 1, (6, 7))
                context(s)

            def attention1():
                s = at[1]

                def t1(i):
                    act.wait_ge(s.a, i + 1)
                    copy(T1_sb[:], psum[2][:, 0:2 * R]).then_inc(s.a_ev, 1)

                def m(i):
                    act.wait_ge(s.m, i + 1)
                    copy(M_sb[:], psum[4][:, 0:4 * R].rearrange("p (c r) -> p c r", c=NCH)).then_inc(s.m_ev, 1)

                def body(i, first=False, final=False):
                    keys(s, i, 0, 2)
                    if not first:
                        exps(s, i - 1, 0)
                    keys(s, i, 1, 3)
                    if not first:
                        exps(s, i - 1, 1)
                    queries(s, i)
                    if not first:
                        transposed(s, i - 1, (0, 1))
                    if not final:
                        t1(i + 1)
                    out_weights(s, i, 3)
                    if not final:
                        m(i + 1)

                t1(0)
                m(0)
                body(0, first=True)
                with act.Fori(1, HP - 1) as i:
                    body(i)
                body(HP - 1, final=True)
                exps(s, HP - 1, 0)
                exps(s, HP - 1, 1)
                transposed(s, HP - 1, (0, 1))
                context(s)

            def experts(n):
                s = ff[n]
                act.wait_ge(s.route, 1)
                nr = (E0, E1)[n]
                nc.scalar.activation(rt[0][:, :, 0:nr], rt[0][:, :, 0:nr], ACT.Exp).then_inc(s.silu, 1)

                def body(i, first=False):
                    for h in range(2):
                        act.wait_ge(s.gu, 4 * i + 2 * h + 1)
                        if not first:
                            act.wait_ge(s.h, 2 * i + h - 1)
                        nc.scalar.activation(silu[:, h, :], psum[2 * h][:], ACT.Silu).then_inc(s.silu, 1)

                body(0, first=True)
                with act.Fori(1, EXPERTS[n]) as i:
                    body(i)

            act.wait_ge(const_loaded, 16 * 8)
            nc.scalar.activation(tgate[:], gate[:], ACT.Tanh).then_inc(gate_ready, 1)
            layer_norm(0)
            attention0()
            layer_norm(1)
            experts(0)
            layer_norm(2)
            attention1()
            layer_norm(3)
            experts(1)

        @block.vector
        def _(dve):
            V = nc.vector

            def layer_norm(n, arrived):
                s = ln[n]
                for t in range(NT):
                    arrived(t)
                    V.bn_stats(stats[:, t, :], X[:, t, :]).then_inc(s.stat, 1)
                for t in range(NT):
                    dve.wait_ge(s.stat, t + 1)
                    V.bn_aggr(meanvar[:, t, :], stats[:, t, :]).then_inc(s.agg, 1)
                dve.wait_ge(s.agg, NT)
                count = [0]

                def link(op):
                    count[0] += 1
                    op.then_inc(s.rstd, 1)
                    dve.wait_ge(s.rstd, count[0])

                link(V.tensor_scalar(varep[:], meanvar[:, :, 1], EPS_LN, None, ALU.add))
                link(V.tensor_scalar(rstd[:].bitcast(I32), varep[:].bitcast(I32), 1, None, ALU.arith_shift_right))
                link(V.tensor_scalar(rstd[:].bitcast(I32), rstd[:].bitcast(I32), -1.0, float(RSQRT_GUESS),
                                     ALU.mult, ALU.add))
                for _ in range(3):
                    link(V.scalar_tensor_tensor(newton[:], rstd[:], -0.5, rstd[:], ALU.mult, ALU.mult))
                    link(V.tensor_tensor(newton[:], newton[:], varep[:], ALU.mult))
                    link(V.scalar_tensor_tensor(rstd[:], newton[:], 1.5, rstd[:], ALU.add, ALU.mult))
                for t in range(NT):
                    V.tensor_scalar(xn[:, t, :], X[:, t, :], meanvar[:, t, 0:1], rstd[:, t:t + 1],
                                    ALU.subtract, ALU.mult).then_inc(s.xn, 1)

            def rope_context():
                dve.wait_ge(kv_loaded, 16 * 7)
                nb = NB
                by_b = lambda a: a.rearrange("p (b l) -> p b l", b=nb)
                wide = lambda tbl: tbl[:].unsqueeze(1).to_broadcast([P, nb, L])
                V.tensor_tensor(by_b(ropeA[:]), by_b(kvT_s), wide(cosT_s), ALU.mult).then_inc(kv_step, 1)
                V.tensor_tensor(by_b(ropeB[:]), by_b(kvTrot_s), wide(sinT_s), ALU.mult).then_inc(kv_step, 1)
                dve.wait_ge(kv_step, 2)
                V.tensor_tensor(kvrT[:], ropeA[:], ropeB[:], ALU.add).then_inc(kv_ready, 1)
                dve.wait_ge(kv_ready, 1)
                V.tensor_tensor(by_b(ropeA[:]), by_b(kv_s), wide(cosR_s), ALU.mult).then_inc(kv_step, 1)
                hd = DC // 2
                for lo, hi in ((0, hd), (hd, 0)):
                    V.tensor_tensor(by_b(ropeB[:])[:, :, lo:lo + hd], by_b(kv_s)[:, :, hi:hi + hd],
                                    sinR_s[:, lo:lo + hd].unsqueeze(1).to_broadcast([P, nb, hd]), ALU.mult)\
                        .then_inc(kv_step, 1)
                dve.wait_ge(kv_step, 5)
                dve.wait_ge(zeros_ready, 1)
                V.tensor_tensor(vbd[0:L, :, 0:DC], by_b(ropeA[:])[0:L], by_b(ropeB[:])[0:L], ALU.add)
                V.tensor_tensor(vbd[L:P, :, DC:2 * DC], by_b(ropeA[:])[L:P], by_b(ropeB[:])[L:P], ALU.add)\
                    .then_inc(kv_ready, 1)

            def softmax_shift(s, i):
                for h in range(2):
                    dve.wait_ge(s.s, 2 * i + h + 1)
                    sc = psum[6 + h][:].rearrange("p (t a l) -> p t a l", t=4, a=2)
                    mx = rowmax[:, 4 * h:4 * h + 4, :]
                    V.tensor_reduce(mx, sc, AX, ALU.max).then_inc(s.max, 1)
                    dve.wait_ge(s.max, 2 * i + h + 1)
                    V.tensor_tensor(probs[:, 4 * h:4 * h + 4], sc, mx.unsqueeze(3).to_broadcast([P, 4, 2, L]),
                                    ALU.subtract).then_inc(s.sub, 1)

            def softmax_sums(s, i):
                for h in range(2):
                    dve.wait_ge(s.exp, 2 * i + h + 1)
                    V.tensor_reduce(rowsum[:, 4 * h:4 * h + 4, :], probs[:, 4 * h:4 * h + 4], AX, ALU.add)\
                        .then_inc(s.sum, 1)
                for h in range(2):
                    dve.wait_ge(s.sum, 2 * i + h + 1)
                    V.reciprocal(rowrec[:, 4 * h:4 * h + 4, :], rowsum[:, 4 * h:4 * h + 4, :]).then_inc(s.rec, 1)

            def add_output(s, g):
                for t in range(NT):
                    dve.wait_ge(s.o, t + 1)
                    V.scalar_tensor_tensor(X[:, t, :], psum[t][:, 0:DM], tgate[:, g:g + 1], X[:, t, :],
                                           ALU.mult, ALU.add).then_inc(s.x, 1)

            def attention0():
                s = at[0]

                def rope(i, n):
                    h, j = divmod(n, 3)
                    dve.wait_ge(s.q, 6 * i + n + 1)
                    src = psum[n][:].rearrange("p (b s) -> p b s", s=S)
                    for dst, tbl, last in ((qc, cosQ_s, False), (qs, sinQ_s, True)):
                        o = V.tensor_tensor(dst[:, j, h * HALF:(h + 1) * HALF].rearrange("p (b s) -> p b s", s=S),
                                            src, tbl[:, j, :].unsqueeze(1).to_broadcast([P, HALF // S, S]), ALU.mult)
                        if last:
                            o.then_inc(s.q_ev, 1)

                def body(i, first=False):
                    if not first:
                        softmax_shift(s, i - 1)
                    for n in range(3):
                        rope(i, n)
                    if not first:
                        softmax_sums(s, i - 1)
                    for n in range(3, 6):
                        rope(i, n)

                body(0, first=True)
                with dve.Fori(1, HP) as i:
                    body(i)
                softmax_shift(s, HP - 1)
                softmax_sums(s, HP - 1)
                add_output(s, 0)

            def attention1():
                s = at[1]
                with dve.Fori(0, HP) as i:
                    softmax_shift(s, i)
                    softmax_sums(s, i)
                add_output(s, 1)

            def routing(n):
                s, nr, g = ff[n], (E0, E1)[n], 2 + n
                a, b, c, d = (r[:, :, 0:nr] for r in rt)
                m1, m2, i1, i2, den, sc = rs
                full = lambda v: v[:].unsqueeze(2).to_broadcast([P, NT, nr])
                row = lambda v: v[:, 0:nr].unsqueeze(1).to_broadcast([P, NT, nr])
                step = sem(f"route{n}_step")
                count = [0]

                def link(op):
                    count[0] += 1
                    op.then_inc(step, 1)
                    dve.wait_ge(step, count[0])

                dve.wait_ge(s.logits, 1)
                lg = psum[7][:, 0:NT * nr].rearrange("p (t e) -> p t e", e=nr)
                if n:
                    link(V.tensor_tensor(a, lg, row(bias_s), ALU.add))
                else:
                    link(V.tensor_copy(a, lg))
                link(V.tensor_reduce(m1[:], a, AX, ALU.max))
                V.tensor_tensor(a, a, full(m1), ALU.subtract).then_inc(s.route, 1)
                dve.wait_ge(s.silu, 1)
                link(V.tensor_reduce(den[:], a, AX, ALU.add))
                link(V.reciprocal(den[:], den[:]))
                link(V.tensor_tensor(a, a, full(den), ALU.mult))
                for mx, idx in ((m1, i1), (m2, i2)):
                    link(V.tensor_reduce(mx[:], a, AX, ALU.max))
                    link(V.tensor_tensor(b, a, full(mx), ALU.is_lt))
                    link(V.scalar_tensor_tensor(b, b, float(E1), row(iota), ALU.mult, ALU.add))
                    link(V.tensor_reduce(idx[:], b, AX, ALU.min))
                    dst = c if mx is m1 else d
                    link(V.tensor_tensor(dst, row(iota), full(idx), ALU.is_equal))
                    if mx is m1:
                        link(V.scalar_tensor_tensor(a, c, -BIG, a, ALU.mult, ALU.add))
                link(V.tensor_tensor(c, c, full(m1), ALU.mult))
                link(V.tensor_tensor(d, d, full(m2), ALU.mult))
                link(V.tensor_tensor(c, c, d, ALU.add))
                link(V.tensor_tensor(den[:], m1[:], m2[:], ALU.add))
                if n:
                    link(V.tensor_scalar(den[:], den[:], EPS_TOPK, None, ALU.add))
                link(V.reciprocal(den[:], den[:]))
                link(V.tensor_scalar(den[:], den[:], tgate[:, g:g + 1], None, ALU.mult))
                if n:
                    link(V.tensor_scalar(coef[:, :, nr], coef[:, :, nr], tgate[:, g:g + 1], None, ALU.mult))
                link(V.tensor_tensor(coef[:, :, 0:nr], c, full(den), ALU.mult))

            def experts(n):
                s, ne = ff[n], EXPERTS[n]
                routing(n)

                def hidden(i, u):
                    for h in range(2):
                        dve.wait_ge(s.gu, 4 * i + 2 * h + 2)
                        dve.wait_ge(s.silu, 2 * i + h + 2)
                        V.tensor_tensor(hT[u][:, h * HALF:(h + 1) * HALF], silu[:, h, :], psum[2 * h + 1][:],
                                        ALU.mult).then_inc(s.h, 1)

                def add(i):
                    for t in range(NT):
                        dve.wait_ge(s.d, NT // 2 * i + t // 2 + 1)
                        if not isinstance(i, int) or i > 0:
                            dve.wait_ge(s.x, NT * (i - 1) + t + 1)
                        V.scalar_tensor_tensor(X[:, t, :], psum[4 + t // 2][:, (t % 2) * DM:(t % 2 + 1) * DM],
                                               coef[:, t, bass.ds(i, 1)], X[:, t, :], ALU.mult, ALU.add)\
                            .then_inc(s.x, 1)

                hidden(0, 0)
                hidden(1, 1)
                add(0)
                with dve.Fori(0, (ne - 2) // 2) as j:
                    for k in range(2):
                        hidden(2 * j + 2 + k, k)
                        add(2 * j + 1 + k)
                if ne % 2:
                    hidden(ne - 1, 0)
                    add(ne - 2)
                add(ne - 1)

            def rope_after_load():
                dve.wait_ge(const_loaded, 16 * 8)

            layer_norm(0, lambda t: dve.wait_ge(x_loaded[t // 4], 16))
            rope_context()
            rope_after_load()
            dve.wait_ge(gate_ready, 1)
            dve.wait_ge(zeros_ready, 3)
            attention0()
            layer_norm(1, lambda t: dve.wait_ge(at[0].x, t + 1))
            experts(0)
            layer_norm(2, lambda t: dve.wait_ge(ff[0].x, NT * (EXPERTS[0] - 1) + t + 1))
            attention1()
            layer_norm(3, lambda t: dve.wait_ge(at[1].x, t + 1))
            experts(1)


def rope_tables(length, dim):
    inv = (1.0 / 10000.0 ** (np.arange(0, dim, 2, dtype=np.float32) / np.float32(dim))).astype(np.float32)
    f = np.arange(length, dtype=np.float32)[:, None] * inv[None, :]
    return np.repeat(np.sin(f), 2, axis=-1), np.repeat(np.cos(f), 2, axis=-1)


def layouts(a):
    f = {k: np.asarray(v) for k, v in a.items()}
    d = {"x": f["x"].reshape(TOK, DM)}
    ctx = f["ctx_512"]
    kvT = np.transpose(ctx, (2, 0, 1)).reshape(DC, TOK)
    hd = DC // 2
    d["kvT"] = np.concatenate([kvT, kvT])
    rot = np.concatenate([kvT[hd:], kvT[:hd]])
    d["kvTrot"] = np.concatenate([rot, rot])
    kv = np.transpose(ctx, (1, 0, 2)).reshape(L, NB * DC)
    d["kv"] = np.concatenate([kv, kv])
    sin, cos = rope_tables(L, DC)
    sign = np.where(np.arange(DC) < hd, -1.0, 1.0).astype(np.float32)
    d["cosT"] = np.concatenate([cos.T, cos.T])
    d["sinT"] = np.concatenate([(sin * sign).T] * 2)
    d["cosR"] = np.concatenate([cos, cos])
    d["sinR"] = np.concatenate([sin * sign] * 2)
    sin, cos = rope_tables(S, DQ)
    half = DQ // 2
    to = (np.arange(DQ) + half) % DQ
    sg = np.where(np.arange(DQ) < half, 1.0, -1.0).astype(np.float32)
    sinp = (sin[:, to] * sg).T
    cosp = cos.T
    stack = lambda m: np.stack([m[0:P], m[0:P], np.concatenate([m[P:DQ], m[P:DQ]])], axis=1)
    d["cosQ"], d["sinQ"] = stack(cosp), stack(sinp)

    def pairs(w):
        return w.reshape(HP, 2, *w.shape[1:])

    for n in range(2):
        g = lambda k: f[f"L{n}_xattn_{k}"]
        wq = pairs(g("Wq").reshape(H, K, DM))
        wcq, wck = pairs(g("w_kc_q")), pairs(g("w_kc_kv"))
        wqr, wkr = pairs(g("W_qr")), pairs(g("W_kr"))
        wo = pairs(np.transpose(g("Wo").reshape(DM, H, K), (1, 2, 0)))
        side = lambda w: np.transpose(w, (0, 2, 1, 3)).reshape(HP, w.shape[2], -1)
        kr = np.zeros((HP, P, 2 * R), np.float32)
        kr[:, 0:DC] = side(wkr)
        if n == 0:
            wqrs = wqr[:, :, to]
            bd = [np.zeros((HP, P, 2 * R), np.float32) for _ in range(2)]
            for m, w in zip(bd, (wqr, wqrs)):
                m[:, 0:DQ - P, 0:R] = w[:, 0, P:]
                m[:, DQ - P:P, R:] = w[:, 1, P:]
            cols = [side(wq), side(wcq), side(wqr[:, :, 0:P]), side(wqrs[:, :, 0:P]), *bd, kr, side(wo), side(wck)]
        else:
            chunks = np.zeros((HP, P, 2, 2, K), np.float32)
            qr = np.zeros((HP, P, 2, 2, R), np.float32)
            chunks[:, 0:QH] = np.transpose(wcq.reshape(HP, 2, K, 2, QH), (0, 4, 1, 3, 2))
            qr[:, 0:QH] = np.transpose(wqr.reshape(HP, 2, 2, QH, R), (0, 3, 1, 2, 4))
            cols = [side(wq), chunks.reshape(HP, P, -1), qr.reshape(HP, P, -1), kr, side(wo), side(wck)]
        d[f"attn{n}"] = np.concatenate(cols, axis=2)

    def expert_pack(wg, wu, wd):
        e = wg.shape[0]
        chunk = lambda w: np.transpose(w.reshape(e, NCH, P, INTER), (0, 2, 1, 3)).reshape(e, P, -1)
        return np.concatenate([chunk(wg), chunk(wu), wd], axis=2)

    gu = f["L0_ffn_expert_gate_up"]
    d["ffn0"] = expert_pack(gu[:, :, 0::2], gu[:, :, 1::2], f["L0_ffn_expert_down"])
    d["ffn1"] = expert_pack(*(np.concatenate([f[f"L1_ffn_{k}"], f[f"L1_ffn_s{k}"][None]]) for k in ("Wg", "Wu", "Wd")))
    router = lambda w: np.transpose(w.T.reshape(NCH, P, -1), (1, 0, 2))
    d["router0"], d["router1"] = router(f["L0_ffn_router_gate"]), router(f["L1_ffn_Wr"])
    rows = lambda v: np.broadcast_to(v[None], (P, v.shape[0]))
    d["bias1"] = rows(f["L1_ffn_bias"])
    d["gates"] = rows(np.concatenate([f["g_xattn"], f["g_ffn"]]))
    d["ident_d"] = np.eye(P, dtype=np.float32)
    d["iota_d"] = rows(np.arange(E1, dtype=np.float32))
    return {k: np.ascontiguousarray(v, dtype=np.float32) for k, v in d.items()}


def kernel(**inputs):
    import concourse.bacc as bacc
    from concourse.bass_utils import run_bass_kernel_spmd

    nc = bacc.Bacc("TRN2", target_bir_lowering=False, num_devices=1)
    arrays = layouts(inputs)
    aps = {k: nc.dram_tensor(k, v.shape, F32, kind="ExternalInput").ap() for k, v in arrays.items()}
    out = nc.dram_tensor("out", (TOK, DM), F32, kind="ExternalOutput").ap()
    build(nc, out=out, **aps)
    r = run_bass_kernel_spmd(nc, [arrays], core_ids=[0])
    return r.results[0]["out"].reshape(NB, S, DM)
```

```python
from contextlib import ExitStack

import numpy as np

import concourse.bass as bass
from concourse import mybir

P = 128
NB, S, DM = 16, 64, 256
L, DC = 64, 64
H, K, DQ, R = 16, 128, 192, 64
HP = H // 2
TOK = NB * S
NT = TOK // P
NCH = DM // P
HALF = 512
E0, E1 = 8, 16
INTER = 128
EPS_LN, EPS_TOPK = 1e-5, 1e-9
RSQRT_GUESS = 0x5F3759DF
NEWTON_OPS = 12
BIG = 4.0

F32 = mybir.dt.float32
F32R = mybir.dt.float32r
I32 = mybir.dt.int32
ALU = mybir.AluOpType
ACT = mybir.ActivationFunctionType
AX = mybir.AxisListType.X

QH = DQ // 2
GU = 4 * INTER
PACKF = GU + DM


def columns(*widths):
    return [sum(widths[:n]) for n in range(len(widths) + 1)]


WQ0, WCQ0, WQR0, WKR0, WO0, WCK0, PACK0 = columns(2 * DM, 2 * DQ, 3 * P, 2 * DC, 2 * DM, 2 * DC)
WQ1, WCQ1, WQR1, WKR1, WO1, WCK1, PACK1 = columns(2 * DM, 4 * K, 2 * QH, 2 * DC, 2 * DM, 2 * DC)


def build(nc, x, kvT, kvTrot, kv, cosT, sinT, cosR, sinR, cosQ, sinQ, attn0, attn1, ffn0, ffn1,
          router0, router1, bias1, gates, ident_d, iota_d, out):
    with ExitStack() as ctx:
        def sb(name, shape, dt=F32):
            return ctx.enter_context(nc.sbuf_tensor(name, shape, dt))

        def split(name, shape):
            return [sb(f"{name}_{part}", shape, F32R) for part in ("hi", "lo")]

        def sem(name):
            return ctx.enter_context(nc.semaphore(name))

        X = sb("X", [P, NT, DM])
        xn = sb("xn", [P, NT, DM])
        xnT = sb("xnT", [P, NCH, TOK])
        xs = split("xs", [P, NCH, TOK])
        ident = sb("ident", [P, P])
        kbd = sb("kbd", [P, NB, 2 * L])
        vbd = sb("vbd", [P, NB, 2 * DC])
        W = [sb(f"W{u}", [P, max(PACK0, PACK1)]) for u in range(2)]
        WF = [sb(f"WF{u}", [P, PACKF]) for u in range(2)]
        stats = sb("stats", [P, NT, 6])
        meanvar = sb("meanvar", [P, NT, 2])
        rstd, varep, newton = sb("rstd", [P, NT]), sb("varep", [P, NT]), sb("newton", [P, NT])
        gate = sb("gate", [P, 4])
        tgate = sb("tgate", [P, 4])
        wr = [sb("wr0", [P, NCH, E0]), sb("wr1", [P, NCH, E1])]
        bias_s = sb("bias_s", [P, E1])
        iota = sb("iota", [P, E1])
        coef = sb("coef", [P, NT, E1 + 1])
        rt = [sb(f"rt{n}", [P, NT, E1]) for n in range(4)]
        rs = [sb(f"rs{n}", [P, NT]) for n in range(5)]

        cosT_s, sinT_s = sb("cosT_s", [P, L]), sb("sinT_s", [P, L])
        cosR_s, sinR_s = sb("cosR_s", [P, DC]), sb("sinR_s", [P, DC])
        cosQ_s, sinQ_s = sb("cosQ_s", [P, 3, S]), sb("sinQ_s", [P, 3, S])
        A = split("A", [P, NCH, 2 * DQ])
        qc = sb("qc", [P, 2, TOK])
        qs = sb("qs", [P, 2, TOK])
        qb = sb("qb", [P, 2, TOK])
        G = sb("G", [P, TOK])
        probs = sb("probs", [P, NT, 2, L])
        rowmax = sb("rowmax", [P, NT, 2])
        rowsum = sb("rowsum", [P, NT, 2])
        rowrec = sb("rowrec", [P, NT, 2])
        PT = sb("PT", [P, HP, TOK])
        N_sb = sb("N_sb", [P, HP, DM])
        Wp = sb("Wp", [P, 3, 2 * DC])
        T1 = sb("T1", [P, 2 * DC])
        M = split("M", [P, NCH, 2 * DC])
        kvT_s, kvTrot_s, kv_s = qc[:, 0, :], qc[:, 1, :], qs[:, 0, :]
        ropeA, ropeB = qb[:, 0, :], qb[:, 1, :]
        WG = [split(f"WG{u}", [P, GU]) for u in range(2)]
        WD = [split(f"WD{u}", [P, DM]) for u in range(2)]
        silu = sb("silu", [P, 2, HALF])
        hid = sb("hid", [P, 2, HALF])
        hT = [split(f"hT{u}", [P, TOK]) for u in range(2)]
        psum = [ctx.enter_context(nc.psum_tensor(f"ps{n}", [P, HALF], F32)) for n in range(8)]

        x_loaded = [sem(f"x_loaded{k}") for k in range(2)]
        const_loaded, kv_loaded, ident_loaded = sem("const_loaded"), sem("kv_loaded"), sem("ident_loaded")
        gate_ready, zeros_ready = sem("gate_ready"), sem("zeros_ready")
        kv_step, kv_ready = sem("kv_step"), sem("kv_ready")
        out_written = sem("out_written")

        block = ctx.enter_context(nc.Block())

        class LnSems:
            def __init__(s, n):
                s.stat = sem(f"ln{n}_stat")
                s.agg = sem(f"ln{n}_agg")
                s.rstd = sem(f"ln{n}_rstd")
                s.xn = sem(f"ln{n}_xn")
                s.tp = sem(f"ln{n}_tp")
                s.hi = sem(f"ln{n}_hi")
                s.lo = sem(f"ln{n}_lo")

        class AttnSems:
            def __init__(s, n):
                p = f"at{n}_"
                s.w = [sem(f"{p}w{u}") for u in range(2)]
                s.a, s.a_hi, s.a_ev = sem(p + "a"), sem(p + "a_hi"), sem(p + "a_ev")
                s.wp, s.wp_ev = sem(p + "wp"), sem(p + "wp_ev")
                s.t1, s.t1_ev = sem(p + "t1"), sem(p + "t1_ev")
                s.m, s.m_hi, s.m_ev = sem(p + "m"), sem(p + "m_hi"), sem(p + "m_ev")
                s.n, s.n_ev = sem(p + "n"), sem(p + "n_ev")
                s.q, s.q_ev = sem(p + "q"), sem(p + "q_ev")
                s.g, s.g_ev = sem(p + "g"), sem(p + "g_ev")
                s.s = sem(p + "s")
                s.max, s.sub = sem(p + "max"), sem(p + "sub")
                s.exp, s.sum = sem(p + "exp"), sem(p + "sum")
                s.rec, s.p = sem(p + "rec"), sem(p + "p")
                s.t, s.t_ev = sem(p + "t"), sem(p + "t_ev")
                s.c, s.c_ev = sem(p + "c"), sem(p + "c_ev")
                s.o, s.x = sem(p + "o"), sem(p + "x")

        class FfnSems:
            def __init__(s, n):
                p = f"ff{n}_"
                s.w = [sem(f"{p}w{u}") for u in range(2)]
                s.ghi, s.wg = sem(p + "ghi"), sem(p + "wg")
                s.dhi, s.wd = sem(p + "dhi"), sem(p + "wd")
                s.logits, s.route, s.rexp = sem(p + "logits"), sem(p + "route"), sem(p + "rexp")
                s.gu = sem(p + "gu")
                s.silu, s.hid = sem(p + "silu"), sem(p + "hid")
                s.hhi, s.h = sem(p + "hhi"), sem(p + "h")
                s.d, s.x = sem(p + "d"), sem(p + "x")

        ln = [LnSems(n) for n in range(4)]
        at = [AttnSems(n) for n in range(2)]
        ff = [FfnSems(n) for n in range(2)]
        EXPERTS = [E0, E1 + 1]

        @block.sync
        def _(sp):
            def row(a, n):
                return a[bass.ds(n, 1)].rearrange("a p c -> (a p) c")

            xv = x.rearrange("(t p) d -> p t d", p=P)
            for k in range(2):
                sp.dma_start(X[:, 4 * k:4 * k + 4, :], xv[:, 4 * k:4 * k + 4, :]).then_inc(x_loaded[k], 16)
            sp.dma_start(ident[:], ident_d).then_inc(ident_loaded, 16)
            sp.dma_start(W[0][:, 0:PACK0], attn0[0]).then_inc(at[0].w[0], 16)
            for dst, src in ((kvT_s, kvT), (kvTrot_s, kvTrot), (kv_s, kv), (cosT_s[:], cosT),
                             (sinT_s[:], sinT), (cosR_s[:], cosR), (sinR_s[:], sinR)):
                sp.dma_start(dst, src).then_inc(kv_loaded, 16)
            for dst, src in ((cosQ_s[:], cosQ), (sinQ_s[:], sinQ), (gate[:], gates), (bias_s[:], bias1),
                             (iota[:], iota_d), (wr[0][:], router0), (wr[1][:], router1)):
                sp.dma_start(dst, src).then_inc(const_loaded, 16)
            sp.dma_start(W[1][:, 0:PACK0], attn0[1]).then_inc(at[0].w[1], 16)
            for u in range(2):
                sp.dma_start(WF[u][:], ffn0[u]).then_inc(ff[0].w[u], 16)
            with sp.Fori(0, HP // 2 - 1) as j:
                for u in range(2):
                    sp.wait_ge(at[0].g, 4 * j + 2 * u + 2)
                    sp.dma_start(W[u][:, 0:PACK0], row(attn0, 2 * j + 2 + u)).then_inc(at[0].w[u], 16)
            for u in range(2):
                sp.wait_ge(at[0].g, 2 * (HP - 1 + u))
                sp.dma_start(W[u][:, 0:PACK1], attn1[u]).then_inc(at[1].w[u], 16)
            with sp.Fori(0, (EXPERTS[0] - 2) // 2) as j:
                for u in range(2):
                    sp.wait_ge(ff[0].wd, 2 * j + u + 1)
                    sp.dma_start(WF[u][:], row(ffn0, 2 * j + 2 + u)).then_inc(ff[0].w[u], 16)
            for u in range(2):
                sp.wait_ge(ff[0].wd, EXPERTS[0] - 1 + u)
                sp.dma_start(WF[u][:], ffn1[u]).then_inc(ff[1].w[u], 16)
            with sp.Fori(0, HP // 2 - 1) as j:
                for u in range(2):
                    sp.wait_ge(at[1].s, 4 * j + 2 * u + 2)
                    sp.dma_start(W[u][:, 0:PACK1], row(attn1, 2 * j + 2 + u)).then_inc(at[1].w[u], 16)
            with sp.Fori(0, (EXPERTS[1] - 3) // 2) as j:
                for u in range(2):
                    sp.wait_ge(ff[1].wd, 2 * j + u + 1)
                    sp.dma_start(WF[u][:], row(ffn1, 2 * j + 2 + u)).then_inc(ff[1].w[u], 16)
            sp.wait_ge(ff[1].wd, EXPERTS[1] - 2)
            sp.dma_start(WF[0][:], ffn1[EXPERTS[1] - 1]).then_inc(ff[1].w[0], 16)
            ov = out.rearrange("(t p) d -> p t d", p=P)
            for t in range(NT):
                sp.wait_ge(ff[1].x, NT * (EXPERTS[1] - 1) + t + 1)
                sp.dma_start(ov[:, t, :], X[:, t, :]).then_inc(out_written, 16)
            sp.wait_ge(out_written, 16 * NT)

        @block.gpsimd
        def _(pool):
            nc.gpsimd.memset(vbd[:], 0.0).then_inc(zeros_ready, 1)
            nc.gpsimd.memset(kbd[:], 0.0).then_inc(zeros_ready, 1)
            nc.gpsimd.memset(coef[:], 1.0).then_inc(zeros_ready, 1)

            def normalise(s):
                with pool.Fori(0, HP) as i:
                    for h in range(2):
                        pool.wait_ge(s.rec, 2 * i + h + 1)
                        part = probs[:, 4 * h:4 * h + 4]
                        nc.gpsimd.tensor_tensor(
                            part, part, rowrec[:, 4 * h:4 * h + 4, :].unsqueeze(3).to_broadcast([P, 4, 2, L]),
                            ALU.mult).then_inc(s.p, 1)

            def split_weights(n):
                s = ff[n]

                def gate_up(e, u):
                    pool.wait_ge(s.ghi, e + 1)
                    nc.gpsimd.tensor_tensor(WG[u][1][:], WF[u][:, 0:GU], WG[u][0][:].bitcast(F32),
                                            ALU.subtract).then_inc(s.wg, 1)

                def down(e, u):
                    pool.wait_ge(s.dhi, e + 1)
                    nc.gpsimd.tensor_tensor(WD[u][1][:], WF[u][:, GU:PACKF], WD[u][0][:].bitcast(F32),
                                            ALU.subtract).then_inc(s.wd, 1)

                for e in range(2):
                    gate_up(e, e)
                    down(e, e)
                gate_up(2, 0)
                pairs = (EXPERTS[n] - 3) // 2
                with pool.Fori(0, pairs) as j:
                    for k in (3, 4):
                        gate_up(2 * j + k, k % 2)
                        down(2 * j + k - 1, (k - 1) % 2)
                for e in range(2 * pairs + 3, EXPERTS[n]):
                    gate_up(e, e % 2)
                    down(e - 1, (e - 1) % 2)
                down(EXPERTS[n] - 1, (EXPERTS[n] - 1) % 2)

            normalise(at[0])
            split_weights(0)
            normalise(at[1])
            split_weights(1)

        @block.tensor
        def _(pe):
            def product(dst, lhs, rhs, start=True, stop=True):
                nc.tensor.matmul(dst, lhs[0], rhs[0], start=start, stop=False)
                nc.tensor.matmul(dst, lhs[0], rhs[1], start=False, stop=False)
                return nc.tensor.matmul(dst, lhs[1], rhs[0], start=False, stop=stop)

            def cut(parts, *index):
                return [part[index] for part in parts]

            def transpose_tiles(n, g, banks):
                for b in range(2):
                    for k in range(2):
                        t = 4 * g + 2 * b + k
                        pe.wait_ge(ln[n].xn, t + 1)
                        for c in range(NCH):
                            last = nc.tensor.transpose(psum[banks[b]][:, (2 * c + k) * P:(2 * c + k + 1) * P],
                                                       xn[:, t, c * P:(c + 1) * P], ident[:])
                    last.then_inc(ln[n].tp, 1)

            def score_weights(s, w, bank, wqr, wkr, rows):
                sets = (wkr - wqr) // rows
                for c in range(sets):
                    last = nc.tensor.matmul(psum[bank][0:rows, c * P:(c + 1) * P],
                                            w[:, wqr + c * rows:wqr + (c + 1) * rows], w[:, wkr:wkr + P],
                                            start=True, stop=True)
                last.then_inc(s.wp, 1)

            def out_weights(s, w, bank, wo, wck):
                for a in range(2):
                    last = nc.tensor.matmul(psum[bank][a * DC:(a + 1) * DC, 0:DM],
                                            w[:, wck + a * DC:wck + (a + 1) * DC],
                                            w[:, wo + a * DM:wo + (a + 1) * DM], start=True, stop=True)
                last.then_inc(s.n, 1)

            def scores(s, i):
                for h in range(2):
                    pe.wait_ge(s.g_ev, 2 * i + h + 1)
                    for t in range(4):
                        for b in range(2):
                            tok = (4 * h + t) * P + b * S
                            last = nc.tensor.matmul(psum[6 + h][b * S:(b + 1) * S, t * P:(t + 1) * P],
                                                    G[:, tok:tok + S], kbd[:, 2 * (4 * h + t) + b, :],
                                                    start=True, stop=True)
                    last.then_inc(s.s, 1)

            def transposes(s, i, banks):
                for h in range(2):
                    pe.wait_ge(s.p, 2 * i + h + 1)
                    for t in range(4):
                        last = nc.tensor.transpose(psum[banks[h]][:, t * P:(t + 1) * P],
                                                   probs[:, 4 * h + t].rearrange("p a l -> p (a l)"), ident[:])
                    last.then_inc(s.t, 1)

            def context_and_output(s):
                pe.wait_ge(s.t_ev, 2 * HP)
                for b in range(NB):
                    if b >= 8:
                        pe.wait_ge(s.c_ev, b - 7)
                    nc.tensor.matmul(psum[b % 8][:, :], vbd[:, b, :], PT[:, :, b * S:(b + 1) * S],
                                     start=True, stop=True).then_inc(s.c, 1)
                pe.wait_ge(s.n_ev, HP)
                for t in range(NT):
                    pe.wait_ge(s.c_ev, max(2 * t + 2, t + 9))
                    for p in range(HP):
                        last = nc.tensor.matmul(psum[t][:, 0:DM], PT[:, p, t * P:(t + 1) * P], N_sb[:, p, :],
                                                start=(p == 0), stop=(p == HP - 1))
                    last.then_inc(s.o, 1)

            def attention0():
                s = at[0]

                def query_weights(w):
                    for c in range(NCH):
                        for a in range(2):
                            wq = w[:, WQ0 + a * DM + c * P:WQ0 + a * DM + (c + 1) * P]
                            wcq = WCQ0 + a * DQ
                            nc.tensor.matmul(psum[c][:, a * P:(a + 1) * P], wq, w[:, wcq:wcq + P],
                                             start=True, stop=True)
                            last = nc.tensor.matmul(psum[c][:, 2 * P + a * (DQ - P):2 * P + (a + 1) * (DQ - P)], wq,
                                                    w[:, wcq + P:wcq + DQ], start=True, stop=True)
                        last.then_inc(s.a, 1)

                def query_latents(h):
                    for j in range(3):
                        for c in range(NCH):
                            last = product(psum[3 * h + j][:, :], cut(A, slice(None), c, slice(j * P, (j + 1) * P)),
                                           cut(xs, slice(None), c, slice(h * HALF, (h + 1) * HALF)),
                                           start=(c == 0), stop=(c == NCH - 1))
                        last.then_inc(s.q, 1)

                def body(i, u, count, first=False, final=False):
                    w = W[u]
                    if first:
                        pe.wait_ge(ln[0].lo, 2)
                    pe.wait_ge(s.a_ev, 2 * i + 2)
                    if not first:
                        pe.wait_ge(s.wp_ev, i)
                        pe.wait_ge(s.n_ev, i)
                    query_latents(0)
                    if first:
                        transpose_tiles(0, 1, (6, 7))
                        pe.wait_ge(ln[0].lo, 4)
                    else:
                        pe.wait_ge(s.g_ev, 2 * i)
                    query_latents(1)
                    if not first:
                        transposes(s, i - 1, (6, 7))
                    if not final:
                        pe.wait_ge(s.q_ev, 6 * i + 2)
                        pe.wait_ge(s.w[1 - u], 16 * (count + u))
                        query_weights(W[1 - u])
                    pe.wait_ge(s.q_ev, 6 * i + 4)
                    score_weights(s, w, 3, WQR0, WKR0, P)
                    out_weights(s, w, 2, WO0, WCK0)
                    pe.wait_ge(s.wp_ev, i + 1)
                    for h in range(2):
                        pe.wait_ge(s.q_ev, 6 * i + 5 + h)
                        for k, rows in enumerate((qc, qs, qb)):
                            for a in range(2):
                                last = nc.tensor.matmul(psum[4 + h][a * DC:(a + 1) * DC, :],
                                                        Wp[:, k, a * DC:(a + 1) * DC],
                                                        rows[:, a, h * HALF:(h + 1) * HALF],
                                                        start=(k == 0), stop=(k == 2))
                        last.then_inc(s.g, 1)
                    if first:
                        pe.wait_ge(kv_ready, 2)
                    else:
                        pe.wait_ge(s.t_ev, 2 * i)
                    scores(s, i)

                pe.wait_ge(s.w[0], 16)
                query_weights(W[0])
                body(0, 0, 1, first=True)
                with pe.Fori(0, HP // 2 - 1) as j:
                    body(2 * j + 1, 1, j + 1)
                    body(2 * j + 2, 0, j + 2)
                body(HP - 1, 1, HP // 2, final=True)
                transposes(s, HP - 1, (6, 7))
                context_and_output(s)

            def attention1():
                s = at[1]

                def t1(w):
                    for a in range(2):
                        for c in range(2):
                            last = nc.tensor.matmul(psum[3][:, a * DC:(a + 1) * DC],
                                                    w[0:QH, WCQ1 + (2 * a + c) * K:WCQ1 + (2 * a + c + 1) * K],
                                                    Wp[0:QH, c, a * DC:(a + 1) * DC],
                                                    start=(c == 0), stop=(c == 1))
                    last.then_inc(s.t1, 1)

                def m(w):
                    for c in range(NCH):
                        for a in range(2):
                            last = nc.tensor.matmul(psum[3][:, (2 * c + a) * DC:(2 * c + a + 1) * DC],
                                                    w[:, WQ1 + a * DM + c * P:WQ1 + a * DM + (c + 1) * P],
                                                    T1[:, a * DC:(a + 1) * DC], start=True, stop=True)
                    last.then_inc(s.m, 1)

                def queries(i, h):
                    for c in range(NCH):
                        last = product(psum[4 + h][:, :], cut(M, slice(None), c), cut(xs, slice(None), c, slice(h * HALF, (h + 1) * HALF)),
                                       start=(c == 0), stop=(c == NCH - 1))
                    last.then_inc(s.g, 1)

                def body(i, u, count, first=False, final=False):
                    w = W[u]
                    if not final:
                        pe.wait_ge(s.w[1 - u], 16 * (count + u))
                        if not first:
                            pe.wait_ge(s.n_ev, i)
                        score_weights(s, W[1 - u], 2, WQR1, WKR1, QH)
                    pe.wait_ge(s.m_ev, i + 1)
                    if first:
                        pe.wait_ge(ln[2].lo, 2)
                    else:
                        pe.wait_ge(s.g_ev, 2 * i)
                    queries(i, 0)
                    if first:
                        transpose_tiles(2, 1, (6, 7))
                        pe.wait_ge(ln[2].lo, 4)
                    queries(i, 1)
                    if not final:
                        pe.wait_ge(s.wp_ev, i + 2)
                        t1(W[1 - u])
                        pe.wait_ge(s.wp_ev, i + 2)
                    out_weights(s, w, 2, WO1, WCK1)
                    if not first:
                        transposes(s, i - 1, (0, 1))
                    scores(s, i)
                    if not final:
                        pe.wait_ge(s.t1_ev, i + 2)
                        m(W[1 - u])
                    if not first:
                        pe.wait_ge(s.t_ev, 2 * i)

                body(0, 0, 1, first=True)
                with pe.Fori(0, HP // 2 - 1) as j:
                    body(2 * j + 1, 1, j + 1)
                    body(2 * j + 2, 0, j + 2)
                body(HP - 1, 1, HP // 2, final=True)
                transposes(s, HP - 1, (0, 1))
                context_and_output(s)

            def first_score_weights():
                s = at[1]
                pe.wait_ge(s.w[0], 16)
                pe.wait_ge(ff[0].h, 2 * EXPERTS[0])
                score_weights(s, W[0], 2, WQR1, WKR1, QH)
                pe.wait_ge(s.wp_ev, 1)
                for a in range(2):
                    for c in range(2):
                        last = nc.tensor.matmul(psum[3][:, a * DC:(a + 1) * DC],
                                                W[0][0:QH, WCQ1 + (2 * a + c) * K:WCQ1 + (2 * a + c + 1) * K],
                                                Wp[0:QH, c, a * DC:(a + 1) * DC], start=(c == 0), stop=(c == 1))
                last.then_inc(s.t1, 1)
                pe.wait_ge(s.t1_ev, 1)
                for c in range(NCH):
                    for a in range(2):
                        last = nc.tensor.matmul(psum[3][:, (2 * c + a) * DC:(2 * c + a + 1) * DC],
                                                W[0][:, WQ1 + a * DM + c * P:WQ1 + a * DM + (c + 1) * P],
                                                T1[:, a * DC:(a + 1) * DC], start=True, stop=True)
                last.then_inc(s.m, 1)

            def experts(n):
                s, ne = ff[n], EXPERTS[n]
                nr = (E0, E1)[n]
                l = ln[2 * n + 1]

                def gate_up(i, u, h, first=False):
                    if not first:
                        pe.wait_ge(s.h, 2 * i + h - 1)
                    tk = slice(h * HALF, (h + 1) * HALF)
                    for k in range(2):
                        for c in range(NCH):
                            col = (2 * k + c) * INTER
                            last = product(psum[2 * h + k][:, :], cut(WG[u], slice(None), slice(col, col + INTER)),
                                           cut(xs, slice(None), c, tk), start=(c == 0), stop=(c == NCH - 1))
                        last.then_inc(s.gu, 1)

                def both(i, u):
                    pe.wait_ge(s.wg, i + 1)
                    gate_up(i, u, 0)
                    gate_up(i, u, 1)

                def down(i, u, first=False):
                    pe.wait_ge(s.wd, i + 1)
                    for t in range(NT):
                        if t % 4 == 0:
                            pe.wait_ge(s.h, 2 * i + t // 4 + 1)
                        if t % 2 == 0 and not first:
                            pe.wait_ge(s.x, NT * (i - 1) + t + 2)
                        last = product(psum[4 + t // 2][:, (t % 2) * DM:(t % 2 + 1) * DM],
                                       cut(hT[u], slice(None), slice(t * P, (t + 1) * P)), cut(WD[u], slice(None)))
                        if t % 2:
                            last.then_inc(s.d, 1)

                transpose_tiles(2 * n + 1, 0, (0, 1))
                pe.wait_ge(s.wg, 1)
                pe.wait_ge(l.lo, 2)
                gate_up(0, 0, 0, first=True)
                transpose_tiles(2 * n + 1, 1, (6, 7))
                pe.wait_ge(l.lo, 4)
                gate_up(0, 0, 1, first=True)
                for t in range(NT):
                    for c in range(NCH):
                        last = nc.tensor.matmul(psum[4][:, t * nr:(t + 1) * nr], xnT[:, c, t * P:(t + 1) * P],
                                                wr[n][:, c, :], start=(c == 0), stop=(c == NCH - 1))
                last.then_inc(s.logits, 1)
                both(1, 1)
                pe.wait_ge(s.route, 1)
                down(0, 0, first=True)
                pairs = (ne - 2) // 2
                with pe.Fori(0, pairs) as j:
                    both(2 * j + 2, 0)
                    down(2 * j + 1, 1)
                    both(2 * j + 3, 1)
                    down(2 * j + 2, 0)
                if ne % 2:
                    both(ne - 1, 0)
                    down(ne - 2, 1)
                    down(ne - 1, 0)
                else:
                    down(ne - 1, 1)

            pe.wait_ge(ident_loaded, 16)
            transpose_tiles(0, 0, (6, 7))
            attention0()
            pe.wait_ge(const_loaded, 16 * 7)
            experts(0)
            first_score_weights()
            transpose_tiles(2, 0, (0, 1))
            attention1()
            experts(1)

        @block.scalar
        def _(act):
            def copy(dst, src):
                return nc.scalar.activation(dst, src, ACT.Copy)

            def transposed_tiles(n, g, banks):
                for b in range(2):
                    act.wait_ge(ln[n].tp, 2 * g + b + 1)
                    tk = slice((4 * g + 2 * b) * P, (4 * g + 2 * b + 2) * P)
                    src = psum[banks[b]][:].rearrange("p (c k) -> p c k", c=NCH)
                    if n % 2:
                        copy(xnT[:, :, tk], src)
                    copy(xs[0][:, :, tk], src).then_inc(ln[n].hi, 1)

            def exps(s, i, h):
                act.wait_ge(s.sub, 2 * i + h + 1)
                part = probs[:, 4 * h:4 * h + 4]
                nc.scalar.activation(part, part, ACT.Exp).then_inc(s.exp, 1)

            def queries(s, i):
                for h in range(2):
                    act.wait_ge(s.g, 2 * i + h + 1)
                    copy(G[:, h * HALF:(h + 1) * HALF], psum[4 + h][:]).then_inc(s.g_ev, 1)

            def transposed(s, i, banks):
                for h in range(2):
                    act.wait_ge(s.t, 2 * i + h + 1)
                    copy(PT[:, bass.ds(i, 1), h * HALF:(h + 1) * HALF].rearrange("p a t -> p (a t)"),
                         psum[banks[h]][:]).then_inc(s.t_ev, 1)

            def out_weights(s, i, bank):
                act.wait_ge(s.n, i + 1)
                copy(N_sb[:, bass.ds(i, 1), :].rearrange("p a t -> p (a t)"), psum[bank][:, 0:DM]).then_inc(s.n_ev, 1)

            def score_weights(s, i, bank, rows, sets):
                act.wait_ge(s.wp, i + 1)
                copy(Wp[0:rows, 0:sets, :],
                     psum[bank][0:rows, 0:sets * P].rearrange("p (c d) -> p c d", c=sets)).then_inc(s.wp_ev, 1)

            def context(s):
                for b in range(NB):
                    act.wait_ge(s.c, b + 1)
                    copy(PT[:, :, b * S:(b + 1) * S],
                         psum[b % 8][:].rearrange("p (h s) -> p h s", h=HP)).then_inc(s.c_ev, 1)

            def gate_up_upper(n, e, u, count):
                act.wait_ge(ff[n].w[u], 16 * count)
                copy(WG[u][0][:], WF[u][:, 0:GU]).then_inc(ff[n].ghi, 1)

            def down_upper(n, u):
                copy(WD[u][0][:], WF[u][:, GU:PACKF]).then_inc(ff[n].dhi, 1)

            def first_experts(n):
                for e in range(2):
                    gate_up_upper(n, e, e, 1)
                    down_upper(n, e)

            def attention0():
                s = at[0]

                def query_weights(i):
                    for c in range(NCH):
                        act.wait_ge(s.a, 2 * i + c + 1)
                        copy(A[0][:, c, :], psum[c][:, 0:2 * DQ]).then_inc(s.a_hi, 1)

                def body(i, first=False, final=False):
                    if not first:
                        exps(s, i - 1, 0)
                        exps(s, i - 1, 1)
                        transposed(s, i - 1, (6, 7))
                    if not final:
                        query_weights(i + 1)
                    score_weights(s, i, 3, P, 3)
                    out_weights(s, i, 2)
                    queries(s, i)

                query_weights(0)
                transposed_tiles(0, 1, (6, 7))
                body(0, first=True)
                with act.Fori(1, HP - 1) as i:
                    body(i)
                first_experts(0)
                body(HP - 1, final=True)
                exps(s, HP - 1, 0)
                exps(s, HP - 1, 1)
                transposed(s, HP - 1, (6, 7))
                context(s)

            def t1_and_m(i, which):
                s = at[1]
                if which == 0:
                    act.wait_ge(s.t1, i + 1)
                    copy(T1[:], psum[3][:, 0:2 * DC]).then_inc(s.t1_ev, 1)
                else:
                    act.wait_ge(s.m, i + 1)
                    copy(M[0][:], psum[3][:, 0:4 * DC].rearrange("p (c r) -> p c r", c=NCH)).then_inc(s.m_hi, 1)

            def attention1():
                s = at[1]

                def body(i, first=False, final=False):
                    if not final:
                        score_weights(s, i + 1, 2, QH, 2)
                    if not first:
                        exps(s, i - 1, 0)
                        exps(s, i - 1, 1)
                    else:
                        transposed_tiles(2, 1, (6, 7))
                    queries(s, i)
                    if not final:
                        t1_and_m(i + 1, 0)
                    out_weights(s, i, 2)
                    if not first:
                        transposed(s, i - 1, (0, 1))
                    if not final:
                        t1_and_m(i + 1, 1)

                body(0, first=True)
                with act.Fori(1, HP - 1) as i:
                    body(i)
                first_experts(1)
                body(HP - 1, final=True)
                exps(s, HP - 1, 0)
                exps(s, HP - 1, 1)
                transposed(s, HP - 1, (0, 1))
                context(s)

            def experts(n):
                s = ff[n]
                nr = (E0, E1)[n]

                def gates(i, h, first=False):
                    act.wait_ge(s.gu, 4 * i + 2 * h + 1)
                    if not first:
                        act.wait_ge(s.hid, 2 * i + h - 1)
                    nc.scalar.activation(silu[:, h, :], psum[2 * h][:], ACT.Silu).then_inc(s.silu, 1)

                def hidden_upper(i, u, h):
                    act.wait_ge(s.hid, 2 * i + h + 1)
                    copy(hT[u][0][:, h * HALF:(h + 1) * HALF], hid[:, h, :]).then_inc(s.hhi, 1)

                def body(i, u, count, first=False, gu=True, d=True):
                    gates(i, 0, first)
                    if first:
                        transposed_tiles(2 * n + 1, 1, (6, 7))
                    gates(i, 1, first)
                    if gu:
                        act.wait_ge(s.gu, 4 * i + 4)
                        gate_up_upper(n, i + 2, u, count)
                    hidden_upper(i, u, 0)
                    hidden_upper(i, u, 1)
                    if d and not first:
                        act.wait_ge(s.d, NT // 2 * i)
                        down_upper(n, 1 - u)

                ne = EXPERTS[n]
                transposed_tiles(2 * n + 1, 0, (0, 1))
                body(0, 0, 2, first=True)
                act.wait_ge(s.route, 1)
                nc.scalar.activation(rt[0][:, :, 0:nr], rt[0][:, :, 0:nr], ACT.Exp).then_inc(s.rexp, 1)
                body(1, 1, 2)
                pairs = (ne - 4) // 2
                with act.Fori(0, pairs) as j:
                    body(2 * j + 2, 0, j + 3)
                    body(2 * j + 3, 1, j + 3)
                for i in range(2 * pairs + 2, ne):
                    body(i, i % 2, i // 2 + 2, gu=i + 2 < ne, d=i + 1 < ne)

            transposed_tiles(0, 0, (6, 7))
            act.wait_ge(const_loaded, 16 * 7)
            nc.scalar.activation(tgate[:], gate[:], ACT.Tanh).then_inc(gate_ready, 1)
            attention0()
            experts(0)
            score_weights(at[1], 0, 2, QH, 2)
            t1_and_m(0, 0)
            t1_and_m(0, 1)
            transposed_tiles(2, 0, (0, 1))
            attention1()
            experts(1)

        @block.vector
        def _(dve):
            V = nc.vector

            def normalise(n, g, arrived, lower=None):
                s, tiles = ln[n], range(4 * g, 4 * g + 4)
                for t in tiles:
                    arrived(t)
                    V.bn_stats(stats[:, t, :], X[:, t, :]).then_inc(s.stat, 1)
                for t in tiles:
                    dve.wait_ge(s.stat, t + 1)
                    V.bn_aggr(meanvar[:, t, :], stats[:, t, :]).then_inc(s.agg, 1)
                if lower:
                    lower()
                dve.wait_ge(s.agg, 4 * g + 4)
                count = [NEWTON_OPS * g]

                def link(op):
                    count[0] += 1
                    op.then_inc(s.rstd, 1)
                    dve.wait_ge(s.rstd, count[0])

                y, v, w = (r[:, 4 * g:4 * g + 4] for r in (rstd, varep, newton))
                link(V.tensor_scalar(v, meanvar[:, 4 * g:4 * g + 4, 1], EPS_LN, None, ALU.add))
                link(V.tensor_scalar(y.bitcast(I32), v.bitcast(I32), 1, None, ALU.arith_shift_right))
                link(V.tensor_scalar(y.bitcast(I32), y.bitcast(I32), -1.0, float(RSQRT_GUESS), ALU.mult, ALU.add))
                for _ in range(3):
                    link(V.scalar_tensor_tensor(w, y, -0.5, y, ALU.mult, ALU.mult))
                    link(V.tensor_tensor(w, w, v, ALU.mult))
                    link(V.scalar_tensor_tensor(y, w, 1.5, y, ALU.add, ALU.mult))
                assert count[0] == NEWTON_OPS * (g + 1)
                for t in tiles:
                    V.tensor_scalar(xn[:, t, :], X[:, t, :], meanvar[:, t, 0:1], rstd[:, t:t + 1],
                                    ALU.subtract, ALU.mult).then_inc(s.xn, 1)

            def lower_part(n, g, banks):
                for b in range(2):
                    dve.wait_ge(ln[n].hi, 2 * g + b + 1)
                    tk = slice((4 * g + 2 * b) * P, (4 * g + 2 * b + 2) * P)
                    V.tensor_tensor(xs[1][:, :, tk], psum[banks[b]][:].rearrange("p (c k) -> p c k", c=NCH),
                                    xs[0][:, :, tk].bitcast(F32), ALU.subtract).then_inc(ln[n].lo, 1)

            def layer_norm(n, arrived, banks):
                normalise(n, 0, arrived)
                normalise(n, 1, arrived, lower=lambda: lower_part(n, 0, banks))

            def rope_context():
                dve.wait_ge(kv_loaded, 16 * 7)
                nb, hd = NB, DC // 2

                def by_b(a):
                    return a.rearrange("p (b l) -> p b l", b=nb)

                def wide(tbl):
                    return tbl.unsqueeze(1).to_broadcast([P, nb, tbl.shape[1]])

                V.tensor_tensor(by_b(ropeA), by_b(kvT_s), wide(cosT_s[:]), ALU.mult).then_inc(kv_step, 1)
                V.tensor_tensor(by_b(ropeB), by_b(kvTrot_s), wide(sinT_s[:]), ALU.mult).then_inc(kv_step, 1)
                dve.wait_ge(kv_step, 2)
                dve.wait_ge(zeros_ready, 2)
                V.tensor_tensor(kbd[0:DC, :, 0:L], by_b(ropeA)[0:DC], by_b(ropeB)[0:DC], ALU.add).then_inc(kv_step, 1)
                V.tensor_tensor(kbd[DC:P, :, L:2 * L], by_b(ropeA)[DC:P], by_b(ropeB)[DC:P], ALU.add)\
                    .then_inc(kv_ready, 1)
                dve.wait_ge(kv_step, 3)
                dve.wait_ge(kv_ready, 1)
                V.tensor_tensor(by_b(ropeA), by_b(kv_s), wide(cosR_s[:]), ALU.mult).then_inc(kv_step, 1)
                for lo, hi in ((0, hd), (hd, 0)):
                    V.tensor_tensor(by_b(ropeB)[:, :, lo:lo + hd], by_b(kv_s)[:, :, hi:hi + hd],
                                    wide(sinR_s[:, lo:lo + hd]), ALU.mult).then_inc(kv_step, 1)
                dve.wait_ge(kv_step, 6)
                V.tensor_tensor(vbd[0:L, :, 0:DC], by_b(ropeA)[0:L], by_b(ropeB)[0:L], ALU.add).then_inc(kv_step, 1)
                V.tensor_tensor(vbd[L:P, :, DC:2 * DC], by_b(ropeA)[L:P], by_b(ropeB)[L:P], ALU.add)\
                    .then_inc(kv_ready, 1)
                dve.wait_ge(kv_step, 7)
                dve.wait_ge(kv_ready, 2)

            def softmax_shift(s, i):
                for h in range(2):
                    dve.wait_ge(s.s, 2 * i + h + 1)
                    sc = psum[6 + h][:].rearrange("p (t a l) -> p t a l", t=4, a=2)
                    mx = rowmax[:, 4 * h:4 * h + 4, :]
                    V.tensor_reduce(mx, sc, AX, ALU.max).then_inc(s.max, 1)
                    dve.wait_ge(s.max, 2 * i + h + 1)
                    V.tensor_tensor(probs[:, 4 * h:4 * h + 4], sc, mx.unsqueeze(3).to_broadcast([P, 4, 2, L]),
                                    ALU.subtract).then_inc(s.sub, 1)

            def softmax_sums(s, i):
                for h in range(2):
                    dve.wait_ge(s.exp, 2 * i + h + 1)
                    V.tensor_reduce(rowsum[:, 4 * h:4 * h + 4, :], probs[:, 4 * h:4 * h + 4], AX, ALU.add)\
                        .then_inc(s.sum, 1)
                for h in range(2):
                    dve.wait_ge(s.sum, 2 * i + h + 1)
                    V.reciprocal(rowrec[:, 4 * h:4 * h + 4, :], rowsum[:, 4 * h:4 * h + 4, :]).then_inc(s.rec, 1)

            def add_output(s, g, t):
                dve.wait_ge(s.o, t + 1)
                V.scalar_tensor_tensor(X[:, t, :], psum[t][:, 0:DM], tgate[:, g:g + 1], X[:, t, :],
                                       ALU.mult, ALU.add).then_inc(s.x, 1)
                dve.wait_ge(s.x, t + 1)

            def attention0():
                s = at[0]

                def query_weights_lower(i):
                    for c in range(NCH):
                        dve.wait_ge(s.a_hi, 2 * i + c + 1)
                        V.tensor_tensor(A[1][:, c, :], psum[c][:, 0:2 * DQ], A[0][:, c, :].bitcast(F32),
                                        ALU.subtract).then_inc(s.a_ev, 1)

                def rope(i, n):
                    h, j = divmod(n, 3)
                    dve.wait_ge(s.q, 6 * i + n + 1)
                    tk = slice(h * HALF, (h + 1) * HALF)

                    def times(dst, half, tbl):
                        return V.tensor_tensor(dst.rearrange("p (b s) -> p b s", s=S),
                                               psum[n][half, :].rearrange("p (b s) -> p b s", s=S),
                                               tbl[half, j, :].unsqueeze(1).to_broadcast([dst.shape[0], HALF // S, S]),
                                               ALU.mult)

                    if j < 2:
                        times(qc[:, j, tk], slice(0, P), cosQ_s)
                        last = times(qs[:, j, tk], slice(0, P), sinQ_s)
                    else:
                        for a in range(2):
                            src = slice(a * S, (a + 1) * S)
                            times(qb[0:S, a, tk], src, cosQ_s)
                            last = times(qb[S:P, a, tk], src, sinQ_s)
                    last.then_inc(s.q_ev, 1)

                def body(i, first=False, final=False):
                    if not first:
                        softmax_shift(s, i - 1)
                    for n in range(3):
                        rope(i, n)
                    if not first:
                        softmax_sums(s, i - 1)
                    else:
                        normalise(0, 1, lambda t: dve.wait_ge(x_loaded[1], 16))
                        lower_part(0, 1, (6, 7))
                    for n in range(3, 6):
                        rope(i, n)
                    if not final:
                        query_weights_lower(i + 1)

                query_weights_lower(0)
                body(0, first=True)
                with dve.Fori(1, HP - 1) as i:
                    body(i)
                body(HP - 1, final=True)
                softmax_shift(s, HP - 1)
                softmax_sums(s, HP - 1)

            def m_lower(i):
                s = at[1]
                dve.wait_ge(s.m_hi, i + 1)
                V.tensor_tensor(M[1][:], psum[3][:, 0:4 * DC].rearrange("p (c r) -> p c r", c=NCH),
                                M[0][:].bitcast(F32), ALU.subtract).then_inc(s.m_ev, 1)

            def attention1():
                s = at[1]
                m_lower(1)
                with dve.Fori(0, HP - 2) as i:
                    softmax_shift(s, i)
                    softmax_sums(s, i)
                    m_lower(i + 2)
                for i in (HP - 2, HP - 1):
                    softmax_shift(s, i)
                    softmax_sums(s, i)

            def routing(n):
                s, nr, g = ff[n], (E0, E1)[n], 2 + n
                a, b, c, d = (r[:, :, 0:nr] for r in rt)
                m1, m2, i1, i2, den = rs
                full = lambda v: v[:].unsqueeze(2).to_broadcast([P, NT, nr])
                row = lambda v: v[:, 0:nr].unsqueeze(1).to_broadcast([P, NT, nr])
                step = sem(f"route{n}_step")
                count = [0]

                def link(op):
                    count[0] += 1
                    op.then_inc(step, 1)
                    dve.wait_ge(step, count[0])

                dve.wait_ge(s.logits, 1)
                lg = psum[4][:, 0:NT * nr].rearrange("p (t e) -> p t e", e=nr)
                if n:
                    link(V.tensor_tensor(a, lg, row(bias_s), ALU.add))
                else:
                    link(V.tensor_copy(a, lg))
                link(V.tensor_reduce(m1[:], a, AX, ALU.max))
                V.tensor_tensor(a, a, full(m1), ALU.subtract).then_inc(s.route, 1)
                dve.wait_ge(s.rexp, 1)
                link(V.tensor_reduce(den[:], a, AX, ALU.add))
                link(V.reciprocal(den[:], den[:]))
                link(V.tensor_tensor(a, a, full(den), ALU.mult))
                for mx, idx in ((m1, i1), (m2, i2)):
                    link(V.tensor_reduce(mx[:], a, AX, ALU.max))
                    link(V.tensor_tensor(b, a, full(mx), ALU.is_lt))
                    link(V.scalar_tensor_tensor(b, b, float(E1), row(iota), ALU.mult, ALU.add))
                    link(V.tensor_reduce(idx[:], b, AX, ALU.min))
                    dst = c if mx is m1 else d
                    link(V.tensor_tensor(dst, row(iota), full(idx), ALU.is_equal))
                    if mx is m1:
                        link(V.scalar_tensor_tensor(a, c, -BIG, a, ALU.mult, ALU.add))
                link(V.tensor_tensor(c, c, full(m1), ALU.mult))
                link(V.tensor_tensor(d, d, full(m2), ALU.mult))
                link(V.tensor_tensor(c, c, d, ALU.add))
                link(V.tensor_tensor(den[:], m1[:], m2[:], ALU.add))
                if n:
                    link(V.tensor_scalar(den[:], den[:], EPS_TOPK, None, ALU.add))
                link(V.reciprocal(den[:], den[:]))
                link(V.tensor_scalar(den[:], den[:], tgate[:, g:g + 1], None, ALU.mult))
                if n:
                    link(V.tensor_scalar(coef[:, :, nr], coef[:, :, nr], tgate[:, g:g + 1], None, ALU.mult))
                link(V.tensor_tensor(coef[:, :, 0:nr], c, full(den), ALU.mult))

            def expert_add(n, i, t, chain=False):
                s = ff[n]
                dve.wait_ge(s.d, NT // 2 * i + t // 2 + 1)
                if not isinstance(i, int) or i > 0:
                    dve.wait_ge(s.x, NT * (i - 1) + t + 1)
                V.scalar_tensor_tensor(X[:, t, :], psum[4 + t // 2][:, (t % 2) * DM:(t % 2 + 1) * DM],
                                       coef[:, t, bass.ds(i, 1)], X[:, t, :], ALU.mult, ALU.add).then_inc(s.x, 1)
                if chain:
                    dve.wait_ge(s.x, NT * i + t + 1)

            def experts(n):
                s, ne = ff[n], EXPERTS[n]

                def hidden(i, u):
                    for h in range(2):
                        dve.wait_ge(s.gu, 4 * i + 2 * h + 2)
                        dve.wait_ge(s.silu, 2 * i + h + 1)
                        V.tensor_tensor(hid[:, h, :], silu[:, h, :], psum[2 * h + 1][:], ALU.mult).then_inc(s.hid, 1)
                    for h in range(2):
                        dve.wait_ge(s.hhi, 2 * i + h + 1)
                        V.tensor_tensor(hT[u][1][:, h * HALF:(h + 1) * HALF], hid[:, h, :],
                                        hT[u][0][:, h * HALF:(h + 1) * HALF].bitcast(F32),
                                        ALU.subtract).then_inc(s.h, 1)

                def add(i):
                    for t in range(NT):
                        expert_add(n, i, t)

                lower_part(2 * n + 1, 1, (6, 7))
                hidden(0, 0)
                routing(n)
                hidden(1, 1)
                add(0)
                with dve.Fori(0, (ne - 2) // 2) as j:
                    for k in range(2):
                        hidden(2 * j + 2 + k, k)
                        add(2 * j + 1 + k)
                if ne % 2:
                    hidden(ne - 1, 0)
                    add(ne - 2)

            normalise(0, 0, lambda t: dve.wait_ge(x_loaded[0], 16))
            lower_part(0, 0, (6, 7))
            rope_context()
            dve.wait_ge(const_loaded, 16 * 7)
            attention0()
            dve.wait_ge(gate_ready, 1)
            dve.wait_ge(zeros_ready, 3)
            layer_norm(1, lambda t: add_output(at[0], 0, t), (0, 1))
            experts(0)
            normalise(2, 0, lambda t: expert_add(0, EXPERTS[0] - 1, t, chain=True))
            m_lower(0)
            normalise(2, 1, lambda t: expert_add(0, EXPERTS[0] - 1, t, chain=True),
                      lower=lambda: lower_part(2, 0, (0, 1)))
            lower_part(2, 1, (6, 7))
            attention1()
            layer_norm(3, lambda t: add_output(at[1], 1, t), (0, 1))
            experts(1)
            for t in range(NT):
                expert_add(1, EXPERTS[1] - 1, t)


def rope_tables(length, dim):
    inv = (1.0 / 10000.0 ** (np.arange(0, dim, 2, dtype=np.float32) / np.float32(dim))).astype(np.float32)
    f = np.arange(length, dtype=np.float32)[:, None] * inv[None, :]
    return np.repeat(np.sin(f), 2, axis=-1), np.repeat(np.cos(f), 2, axis=-1)


def layouts(a):
    f = {k: np.asarray(v) for k, v in a.items()}
    d = {"x": f["x"].reshape(TOK, DM)}
    ctx = f["ctx_512"]
    kvT = np.transpose(ctx, (2, 0, 1)).reshape(DC, TOK)
    hd = DC // 2
    d["kvT"] = np.concatenate([kvT, kvT])
    rot = np.concatenate([kvT[hd:], kvT[:hd]])
    d["kvTrot"] = np.concatenate([rot, rot])
    kv = np.transpose(ctx, (1, 0, 2)).reshape(L, NB * DC)
    d["kv"] = np.concatenate([kv, kv])
    sin, cos = rope_tables(L, DC)
    sign = np.where(np.arange(DC) < hd, -1.0, 1.0).astype(np.float32)
    d["cosT"] = np.concatenate([cos.T, cos.T])
    d["sinT"] = np.concatenate([(sin * sign).T] * 2)
    d["cosR"] = np.concatenate([cos, cos])
    d["sinR"] = np.concatenate([sin * sign] * 2)
    sin, cos = rope_tables(S, DQ)
    half = DQ // 2
    to = (np.arange(DQ) + half) % DQ
    sg = np.where(np.arange(DQ) < half, 1.0, -1.0).astype(np.float32)
    sinp = (sin[:, to] * sg).T
    cosp = cos.T
    stack = lambda m: np.stack([m[0:P], m[0:P], np.concatenate([m[P:DQ], m[P:DQ]])], axis=1)
    d["cosQ"], d["sinQ"] = stack(cosp), stack(sinp)

    def pairs(w):
        return w.reshape(HP, 2, *w.shape[1:])

    for n in range(2):
        g = lambda k: f[f"L{n}_xattn_{k}"]
        wq = pairs(g("Wq").reshape(H, K, DM))
        wcq, wck = pairs(g("w_kc_q")), pairs(g("w_kc_kv"))
        wqr, wkr = pairs(g("W_qr")), pairs(g("W_kr"))
        wo = pairs(np.transpose(g("Wo").reshape(DM, H, K), (1, 2, 0)))
        side = lambda w: np.transpose(w, (0, 2, 1, 3)).reshape(HP, w.shape[2], -1)
        kr = np.zeros((HP, 2, R, 2, DC), np.float32)
        for a in range(2):
            kr[:, a, :, a] = np.transpose(wkr[:, a], (0, 2, 1))
        kr = kr.reshape(HP, P, P)
        rt = lambda w: np.transpose(w, (0, 1, 3, 2)).reshape(HP, P, -1)
        if n == 0:
            wqrs = wqr[:, :, to]
            qr = [rt(wqr[:, :, 0:P]), rt(wqrs[:, :, 0:P]), rt(wqr[:, :, P:]), rt(wqrs[:, :, P:])]
            cols = [side(wq), side(wcq), *qr, kr, side(wo), side(wck)]
        else:
            chunks = np.zeros((HP, P, 2, 2, K), np.float32)
            chunks[:, 0:QH] = np.transpose(wcq.reshape(HP, 2, K, 2, QH), (0, 4, 1, 3, 2))
            cols = [side(wq), chunks.reshape(HP, P, -1), rt(wqr), kr, side(wo), side(wck)]
        d[f"attn{n}"] = np.concatenate(cols, axis=2)

    def expert_pack(wg, wu, wd):
        e = wg.shape[0]
        chunk = lambda w: np.transpose(w.reshape(e, NCH, P, INTER), (0, 2, 1, 3)).reshape(e, P, -1)
        return np.concatenate([chunk(wg), chunk(wu), wd], axis=2)

    gu = f["L0_ffn_expert_gate_up"]
    d["ffn0"] = expert_pack(gu[:, :, 0::2], gu[:, :, 1::2], f["L0_ffn_expert_down"])
    d["ffn1"] = expert_pack(*(np.concatenate([f[f"L1_ffn_{k}"], f[f"L1_ffn_s{k}"][None]]) for k in ("Wg", "Wu", "Wd")))
    router = lambda w: np.transpose(w.T.reshape(NCH, P, -1), (1, 0, 2))
    d["router0"], d["router1"] = router(f["L0_ffn_router_gate"]), router(f["L1_ffn_Wr"])
    rows = lambda v: np.broadcast_to(v[None], (P, v.shape[0]))
    d["bias1"] = rows(f["L1_ffn_bias"])
    d["gates"] = rows(np.concatenate([f["g_xattn"], f["g_ffn"]]))
    d["ident_d"] = np.eye(P, dtype=np.float32)
    d["iota_d"] = rows(np.arange(E1, dtype=np.float32))
    return {k: np.ascontiguousarray(v, dtype=np.float32) for k, v in d.items()}


def kernel(**inputs):
    import concourse.bacc as bacc
    from concourse.bass_utils import run_bass_kernel_spmd

    nc = bacc.Bacc("TRN2", target_bir_lowering=False, num_devices=1)
    arrays = layouts(inputs)
    aps = {k: nc.dram_tensor(k, v.shape, F32, kind="ExternalInput").ap() for k, v in arrays.items()}
    out = nc.dram_tensor("out", (TOK, DM), F32, kind="ExternalOutput").ap()
    build(nc, out=out, **aps)
    r = run_bass_kernel_spmd(nc, [arrays], core_ids=[0])
    return r.results[0]["out"].reshape(NB, S, DM)
```

```python
from contextlib import ExitStack

import numpy as np

import concourse.bass as bass
from concourse import mybir

P = 128
NB, S, DM = 16, 64, 256
L, DC = 64, 64
H, K, DQ, R = 16, 128, 192, 64
HP = H // 2
TOK = NB * S
NT = TOK // P
NCH = DM // P
HALF = 512
E0, E1 = 8, 16
INTER = 128
EPS_LN, EPS_TOPK = 1e-5, 1e-9
RSQRT_GUESS = 0x5F3759DF
LN_STEPS = 4 + 12 + 1
BIG = 4.0

F32 = mybir.dt.float32
F32R = mybir.dt.float32r
I32 = mybir.dt.int32
ALU = mybir.AluOpType
ACT = mybir.ActivationFunctionType
AX = mybir.AxisListType.X

QH = DQ // 2
GU = 4 * INTER
PACKF = GU + DM


def columns(*widths):
    return [sum(widths[:n]) for n in range(len(widths) + 1)]


WQ0, WCQ0, WQR0, WKR0, WO0, WCK0, PACK0 = columns(2 * DM, 2 * DQ, 3 * P, 2 * DC, 2 * DM, 2 * DC)
WQ1, WCQ1, WQR1, WKR1, WO1, WCK1, PACK1 = columns(2 * DM, 4 * K, 2 * QH, 2 * DC, 2 * DM, 2 * DC)


def build(nc, x, kvT, kvTrot, kv, cosT, sinT, cosR, sinR, cosQ, sinQ, attn0, attn1, ffn0, ffn1,
          router0, router1, bias1, gates, ident_d, iota_d, out):
    with ExitStack() as ctx:
        def sb(name, shape, dt=F32):
            return ctx.enter_context(nc.sbuf_tensor(name, shape, dt))

        def split(name, shape):
            return [sb(f"{name}_{part}", shape, F32R) for part in ("hi", "lo")]

        def sem(name):
            return ctx.enter_context(nc.semaphore(name))

        X = sb("X", [P, NT, DM])
        xs = split("xs", [P, NCH, TOK])
        ident = sb("ident", [P, P])
        kbd = sb("kbd", [P, NB, 2 * L])
        vbd = split("vbd", [P, NB, 2 * DC])
        W = [sb(f"W{u}", [P, max(PACK0, PACK1)]) for u in range(2)]
        WF = [sb(f"WF{u}", [P, PACKF]) for u in range(2)]
        stats = sb("stats", [P, NT, 6])
        meanvar = sb("meanvar", [P, NT, 2])
        rstd, varep, newton = sb("rstd", [P, NT]), sb("varep", [P, NT]), sb("newton", [P, NT])
        shift = sb("shift", [P, NT])
        gate = sb("gate", [P, 4])
        tgate = sb("tgate", [P, 4])
        wr = [sb("wr0", [P, NCH, E0]), sb("wr1", [P, NCH, E1])]
        bias_s = sb("bias_s", [P, E1])
        iota = sb("iota", [P, E1])
        coef = sb("coef", [P, NT, E1 + 1])
        rs = [sb(f"rs{n}", [P, NT]) for n in range(5)]

        cosT_s, sinT_s = sb("cosT_s", [P, L]), sb("sinT_s", [P, L])
        cosR_s, sinR_s = sb("cosR_s", [P, DC]), sb("sinR_s", [P, DC])
        cosQ_s, sinQ_s = sb("cosQ_s", [P, 3, S]), sb("sinQ_s", [P, 3, S])
        A = split("A", [P, NCH, 2 * DQ])
        qc = sb("qc", [P, 2, TOK])
        qs = sb("qs", [P, 2, TOK])
        qb = sb("qb", [P, 2, TOK])
        G = sb("G", [P, TOK])
        probs = sb("probs", [P, NT, 2, L])
        rowmax = sb("rowmax", [P, NT, 2])
        rowsum = sb("rowsum", [P, NT, 2])
        rowrec = sb("rowrec", [P, NT, 2])
        PT = split("PT", [P, HP, TOK])
        N = split("N", [P, HP, DM])
        Wp = sb("Wp", [P, 3, 2 * DC])
        T1 = sb("T1", [P, 2 * DC])
        M = [part[:, :, 0:2 * DC] for part in A]
        kvT_s, kvTrot_s = probs[:].rearrange("p t a l -> p (t a) l"), G[:].rearrange("p (b l) -> p b l", b=NB)
        kv_s = [WF[u][:, 0:HALF].rearrange("p (b l) -> p b l", b=NB // 2) for u in range(2)]
        rope_s = [kvTrot_s[:, u * NB // 2:(u + 1) * NB // 2] for u in range(2)]
        xn = qb[:].rearrange("p a (t d) -> p (a t) d", d=DM)
        xnT = qs
        hid = qc[:, 0, :].rearrange("p (h t) -> p h t", h=2)
        silu = qc[:, 1, :].rearrange("p (h t) -> p h t", h=2)
        hT = [[part[:, u, :] for part in PT] for u in range(2)]
        rt = [probs[:, n, :, :].rearrange("p a (t e) -> p (a t) e", e=E1) for n in range(4)]
        WG = [split(f"WG{u}", [P, GU]) for u in range(2)]
        WD = [split(f"WD{u}", [P, DM]) for u in range(2)]
        psum = [ctx.enter_context(nc.psum_tensor(f"ps{n}", [P, HALF], F32)) for n in range(8)]

        x_loaded = [sem(f"x_loaded{k}") for k in range(4)]
        query_rope_loaded = sem("query_rope_loaded")
        const_loaded, ident_loaded = sem("const_loaded"), sem("ident_loaded")
        context_cols_loaded, context_rows_loaded = sem("context_cols_loaded"), sem("context_rows_loaded")
        gate_ready, zeros_ready = sem("gate_ready"), sem("zeros_ready")
        context_step = sem("context_step")
        COLS_READY, ROWS_READY = 3, 3 + 4 + 2 + 2
        kbd_ready, vbd_hi, kv_ready = sem("kbd_ready"), sem("vbd_hi"), sem("kv_ready")
        out_written = sem("out_written")

        block = ctx.enter_context(nc.Block())

        class LnSems:
            def __init__(s, n):
                s.stat = sem(f"ln{n}_stat")
                s.rstd = sem(f"ln{n}_rstd")
                s.xn = sem(f"ln{n}_xn")
                s.xn_act = sem(f"ln{n}_xn_act")
                s.tp = sem(f"ln{n}_tp")
                s.hi = sem(f"ln{n}_hi")
                s.lo = sem(f"ln{n}_lo")
                s.whole = sem(f"ln{n}_whole")

        class AttnSems:
            def __init__(s, n):
                p = f"at{n}_"
                s.w = [sem(f"{p}w{u}") for u in range(2)]
                s.wo = [sem(f"{p}wo{u}") for u in range(2)]
                s.a, s.a_hi, s.a_ev = sem(p + "a"), sem(p + "a_hi"), sem(p + "a_ev")
                s.wp, s.wp_ev = sem(p + "wp"), sem(p + "wp_ev")
                s.t1, s.t1_ev = sem(p + "t1"), sem(p + "t1_ev")
                s.m, s.m_hi, s.m_ev = sem(p + "m"), sem(p + "m_hi"), sem(p + "m_ev")
                s.n, s.n_hi, s.n_ev = sem(p + "n"), sem(p + "n_hi"), sem(p + "n_ev")
                s.q, s.q_ev = sem(p + "q"), sem(p + "q_ev")
                s.g, s.g_ev = sem(p + "g"), sem(p + "g_ev")
                s.s = sem(p + "s")
                s.max, s.sub = sem(p + "max"), sem(p + "sub")
                s.exp, s.sum = sem(p + "exp"), sem(p + "sum")
                s.rec, s.p = sem(p + "rec"), sem(p + "p")
                s.t, s.t_hi, s.t_ev = sem(p + "t"), sem(p + "t_hi"), sem(p + "t_ev")
                s.c, s.c_hi, s.c_ev = sem(p + "c"), sem(p + "c_hi"), sem(p + "c_ev")
                s.o, s.x = sem(p + "o"), sem(p + "x")

        class FfnSems:
            def __init__(s, n):
                p = f"ff{n}_"
                s.w = [sem(f"{p}w{u}") for u in range(2)]
                s.ghi, s.wg = sem(p + "ghi"), sem(p + "wg")
                s.dhi, s.wd = sem(p + "dhi"), sem(p + "wd")
                s.logits, s.read = sem(p + "logits"), sem(p + "read")
                s.route, s.rexp = sem(p + "route"), sem(p + "rexp")
                s.gu = sem(p + "gu")
                s.tanh, s.silu, s.hid = sem(p + "tanh"), sem(p + "silu"), sem(p + "hid")
                s.hhi, s.h = sem(p + "hhi"), sem(p + "h")
                s.d, s.x = sem(p + "d"), sem(p + "x")

        ln = [LnSems(n) for n in range(4)]
        at = [AttnSems(n) for n in range(2)]
        ff = [FfnSems(n) for n in range(2)]
        EXPERTS = [E0, E1 + 1]

        @block.sync
        def _(sp):
            def row(a, n):
                return a[bass.ds(n, 1)].rearrange("a p c -> (a p) c")

            def load_query_part(n, u, src):
                cut = (WO0, WO1)[n]
                sp.dma_start(W[u][:, 0:cut], src[:, 0:cut]).then_inc(at[n].w[u], 16)

            def load_output_part(n, u, src):
                cut, end = ((WO0, PACK0), (WO1, PACK1))[n]
                sp.dma_start(W[u][:, cut:end], src[:, cut:end]).then_inc(at[n].wo[u], 16)

            def load_pair(n, u, src):
                load_query_part(n, u, src)
                load_output_part(n, u, src)

            xv = x.rearrange("(t p) d -> p t d", p=P)

            def load_stream(k):
                sp.dma_start(X[:, 2 * k:2 * k + 2, :], xv[:, 2 * k:2 * k + 2, :]).then_inc(x_loaded[k], 16)

            load_stream(0)
            load_stream(1)
            sp.dma_start(ident[:], ident_d).then_inc(ident_loaded, 16)
            load_query_part(0, 0, attn0[0])
            load_stream(2)
            load_stream(3)
            load_output_part(0, 0, attn0[0])
            for dst, src in ((cosQ_s, cosQ), (sinQ_s, sinQ)):
                sp.dma_start(dst[:], src).then_inc(query_rope_loaded, 16)
            for dst, src in ((kvT_s, kvT.rearrange("p (b l) -> p b l", b=NB)), (cosT_s[:], cosT),
                             (kvTrot_s, kvTrot.rearrange("p (b l) -> p b l", b=NB)), (sinT_s[:], sinT)):
                sp.dma_start(dst, src).then_inc(context_cols_loaded, 16)
            for dst, src in (*((kv_s[u], kv.rearrange("p (h b l) -> h p b l", h=2, b=NB // 2)[u]) for u in range(2)),
                             (sinR_s[:], sinR), (cosR_s[:], cosR)):
                sp.dma_start(dst, src).then_inc(context_rows_loaded, 16)
            for dst, src in ((gate[:], gates), (bias_s[:], bias1),
                             (iota[:], iota_d), (wr[0][:], router0), (wr[1][:], router1)):
                sp.dma_start(dst, src).then_inc(const_loaded, 16)
            load_pair(0, 1, attn0[1])
            with sp.Fori(0, HP // 2 - 1) as j:
                for u in range(2):
                    sp.wait_ge(at[0].g, 4 * j + 2 * u + 2)
                    load_pair(0, u, row(attn0, 2 * j + 2 + u))
            sp.wait_ge(kv_ready, 4)
            for u in range(2):
                sp.dma_start(WF[u][:], ffn0[u]).then_inc(ff[0].w[u], 16)
            for u in range(2):
                sp.wait_ge(at[0].g, 2 * (HP - 1 + u))
                load_pair(1, u, attn1[u])
            with sp.Fori(0, (EXPERTS[0] - 2) // 2) as j:
                for u in range(2):
                    sp.wait_ge(ff[0].wd, 2 * j + u + 1)
                    sp.dma_start(WF[u][:], row(ffn0, 2 * j + 2 + u)).then_inc(ff[0].w[u], 16)
            for u in range(2):
                sp.wait_ge(ff[0].wd, EXPERTS[0] - 1 + u)
                sp.dma_start(WF[u][:], ffn1[u]).then_inc(ff[1].w[u], 16)
            with sp.Fori(0, HP // 2 - 1) as j:
                for u in range(2):
                    sp.wait_ge(at[1].m, 2 * j + u + 1)
                    load_query_part(1, u, row(attn1, 2 * j + 2 + u))
                    sp.wait_ge(at[1].n, 2 * j + u + 1)
                    load_output_part(1, u, row(attn1, 2 * j + 2 + u))
            with sp.Fori(0, (EXPERTS[1] - 3) // 2) as j:
                for u in range(2):
                    sp.wait_ge(ff[1].wd, 2 * j + u + 1)
                    sp.dma_start(WF[u][:], row(ffn1, 2 * j + 2 + u)).then_inc(ff[1].w[u], 16)
            sp.wait_ge(ff[1].wd, EXPERTS[1] - 2)
            sp.dma_start(WF[0][:], ffn1[EXPERTS[1] - 1]).then_inc(ff[1].w[0], 16)
            ov = out.rearrange("(t p) d -> p t d", p=P)
            for t in range(NT):
                sp.wait_ge(ff[1].x, NT * (EXPERTS[1] - 1) + t + 1)
                sp.dma_start(ov[:, t, :], X[:, t, :]).then_inc(out_written, 16)
            sp.wait_ge(out_written, 16 * NT)

        @block.gpsimd
        def _(pool):
            nc.gpsimd.memset(kbd[:], 0.0).then_inc(zeros_ready, 1)
            for part in vbd:
                nc.gpsimd.memset(part[:].bitcast(F32), 0.0).then_inc(zeros_ready, 1)
            nc.gpsimd.memset(coef[:], 1.0).then_inc(zeros_ready, 1)

            def rope_context():
                def for_batches(tbl, count):
                    return tbl.unsqueeze(1).to_broadcast([P, count, tbl.shape[1]])

                def step(dst, a, b, op):
                    nc.gpsimd.tensor_tensor(dst, a, b, op).then_inc(context_step, 1)

                hd = DC // 2
                pool.wait_ge(context_cols_loaded, 16 * 4)
                step(kvT_s, kvT_s, for_batches(cosT_s[:], NB), ALU.mult)
                step(kvTrot_s, kvTrot_s, for_batches(sinT_s[:], NB), ALU.mult)
                pool.wait_ge(context_step, 2)
                step(kvT_s, kvT_s, kvTrot_s, ALU.add)
                pool.wait_ge(context_step, 3)
                pool.wait_ge(context_rows_loaded, 16 * 4)
                for u in range(2):
                    for lo, hi in ((0, hd), (hd, 0)):
                        step(rope_s[u][:, :, lo:lo + hd], kv_s[u][:, :, hi:hi + hd],
                             for_batches(sinR_s[:, lo:lo + hd], NB // 2), ALU.mult)
                pool.wait_ge(context_step, 7)
                for u in range(2):
                    step(kv_s[u], kv_s[u], for_batches(cosR_s[:], NB // 2), ALU.mult)
                for u in range(2):
                    pool.wait_ge(context_step, 8 + u)
                    step(kv_s[u], kv_s[u], rope_s[u], ALU.add)

            def vbd_lower():
                pool.wait_ge(zeros_ready, 4)
                pool.wait_ge(vbd_hi, 1)
                for half, cols in ((slice(0, L), slice(0, DC)), (slice(L, P), slice(DC, 2 * DC))):
                    for u in range(2):
                        batches = slice(u * NB // 2, (u + 1) * NB // 2)
                        nc.gpsimd.tensor_tensor(vbd[1][half, batches, cols], kv_s[u][half],
                                                vbd[0][half, batches, cols].bitcast(F32),
                                                ALU.subtract).then_inc(kv_ready, 1)
                pool.wait_ge(kv_ready, 4)

            def normalise(s):
                with pool.Fori(0, HP - 1) as i:
                    for h in range(2):
                        pool.wait_ge(s.rec, 2 * i + h + 1)
                        part = probs[:, 4 * h:4 * h + 4]
                        nc.gpsimd.tensor_tensor(
                            part, part, rowrec[:, 4 * h:4 * h + 4, :].unsqueeze(3).to_broadcast([P, 4, 2, L]),
                            ALU.mult).then_inc(s.p, 1)

            def whole_stream(n, h):
                pool.wait_ge(ln[n].lo, 2 * h + 2)
                hi, lo = (part[:, :, h * HALF:(h + 1) * HALF].bitcast(F32) for part in xs)
                nc.gpsimd.tensor_tensor(xnT[:, :, h * HALF:(h + 1) * HALF], hi, lo, ALU.add).then_inc(ln[n].whole, 1)

            def lower_parts(n):
                s = ff[n]

                def gate_up(e, u):
                    pool.wait_ge(s.ghi, e + 1)
                    nc.gpsimd.tensor_tensor(WG[u][1][:], WF[u][:, 0:GU], WG[u][0][:].bitcast(F32),
                                            ALU.subtract).then_inc(s.wg, 1)

                def down(e, u):
                    pool.wait_ge(s.dhi, e + 1)
                    nc.gpsimd.tensor_tensor(WD[u][1][:], WF[u][:, GU:PACKF], WD[u][0][:].bitcast(F32),
                                            ALU.subtract).then_inc(s.wd, 1)

                def hidden_lower(k, u, h, pair):
                    pool.wait_ge(s.hhi, k + 1)
                    nc.gpsimd.tensor_tensor(hT[u][1][:, h * HALF:(h + 1) * HALF], hid[:, pair, :],
                                            hT[u][0][:, h * HALF:(h + 1) * HALF].bitcast(F32),
                                            ALU.subtract).then_inc(s.h, 1)

                def body(i, u, gu=True, d=True):
                    hidden_lower(2 * i, u, 0, 0)
                    hidden_lower(2 * i + 1, u, 1, 1)
                    if gu:
                        gate_up(i + 2, u)
                    if d:
                        down(i + 1, 1 - u)

                for e in range(2):
                    gate_up(e, e)
                    down(e, e)
                whole_stream(2 * n + 1, 0)
                whole_stream(2 * n + 1, 1)
                hidden_lower(0, 0, 0, 0)
                hidden_lower(1, 1, 0, 1)
                hidden_lower(2, 0, 1, 0)
                gate_up(2, 0)
                gate_up(3, 1)
                hidden_lower(3, 1, 1, 1)
                down(2, 0)
                ne = EXPERTS[n]
                pairs = (ne - 4) // 2
                with pool.Fori(0, pairs) as j:
                    body(2 * j + 2, 0)
                    body(2 * j + 3, 1)
                for i in range(2 * pairs + 2, ne - 1):
                    body(i, i % 2, gu=i + 2 < ne, d=i + 1 < ne)
                hidden_lower(2 * ne - 2, (ne - 1) % 2, 0, 0)

            rope_context()
            vbd_lower()
            normalise(at[0])
            lower_parts(0)
            normalise(at[1])
            lower_parts(1)

        @block.tensor
        def _(pe):
            def product(dst, lhs, rhs, start=True, stop=True):
                nc.tensor.matmul(dst, lhs[0], rhs[0], start=start, stop=False)
                nc.tensor.matmul(dst, lhs[0], rhs[1], start=False, stop=False)
                return nc.tensor.matmul(dst, lhs[1], rhs[0], start=False, stop=stop)

            def bridge(count, bank):
                for _ in range(count):
                    nc.tensor.matmul(psum[bank][:, 0:P], ident[:], ident[:], start=True, stop=True)

            def cut(parts, *index):
                return [part[index] for part in parts]

            def transpose_tiles(n, g, banks):
                for b in range(2):
                    for k in range(2):
                        t = 4 * g + 2 * b + k
                        pe.wait_ge((ln[n].xn, ln[n].xn_act)[b], 2 * g + k + 1)
                        for c in range(NCH):
                            last = nc.tensor.transpose(psum[banks[b]][:, (2 * c + k) * P:(2 * c + k + 1) * P],
                                                       xn[:, t, c * P:(c + 1) * P], ident[:])
                    last.then_inc(ln[n].tp, 1)

            def score_weights(s, w, bank, wqr, wkr, rows):
                sets = (wkr - wqr) // rows
                for c in range(sets):
                    last = nc.tensor.matmul(psum[bank][0:rows, c * P:(c + 1) * P],
                                            w[:, wqr + c * rows:wqr + (c + 1) * rows], w[:, wkr:wkr + P],
                                            start=True, stop=True)
                last.then_inc(s.wp, 1)

            def out_weights(s, w, bank, wo, wck):
                for a in range(2):
                    last = nc.tensor.matmul(psum[bank][a * DC:(a + 1) * DC, 0:DM],
                                            w[:, wck + a * DC:wck + (a + 1) * DC],
                                            w[:, wo + a * DM:wo + (a + 1) * DM], start=True, stop=True)
                last.then_inc(s.n, 1)

            def scores(s, i):
                for h in range(2):
                    pe.wait_ge(s.g_ev, 2 * i + h + 1)
                    for t in range(4):
                        for b in range(2):
                            tok = (4 * h + t) * P + b * S
                            last = nc.tensor.matmul(psum[6 + h][b * S:(b + 1) * S, t * P:(t + 1) * P],
                                                    G[:, tok:tok + S], kbd[:, 2 * (4 * h + t) + b, :],
                                                    start=True, stop=True)
                    last.then_inc(s.s, 1)

            def transposes(s, i, banks):
                for h in range(2):
                    pe.wait_ge(s.p, 2 * i + h + 1)
                    for t in range(4):
                        last = nc.tensor.transpose(psum[banks[h]][:, t * P:(t + 1) * P],
                                                   probs[:, 4 * h + t].rearrange("p a l -> p (a l)"), ident[:])
                    last.then_inc(s.t, 1)

            def context(b, pairs):
                cols = slice(pairs.start * S, pairs.stop * S)
                return product(psum[b % 8][:, cols], cut(vbd, slice(None), b),
                               cut(PT, slice(None), pairs, slice(b * S, (b + 1) * S)))

            def context_and_output(s, n):
                early = 6
                pe.wait_ge(kv_ready, 4)
                pe.wait_ge(s.t_ev, 2 * HP - 2)
                pe.wait_ge(s.n_ev, HP)
                for b in range(early):
                    context(b, slice(0, HP - 1))
                transposes(s, HP - 1, (6, 7))
                pe.wait_ge(s.t_ev, 2 * HP - 1)
                for b in range(NB):
                    if b == 6:
                        pe.wait_ge(s.t_ev, 2 * HP)
                    if b >= 8:
                        pe.wait_ge(s.c_ev, b - 7)
                    context(b, slice(HP - 1, HP) if b < early else slice(0, HP)).then_inc(s.c, 1)
                for t in range(NT):
                    if t == NT - 1:
                        transpose_tiles(n, 0, (0, 1))
                    pe.wait_ge(s.c_ev, max(2 * t + 2, t + 9))
                    for p in range(HP):
                        last = product(psum[t][:, 0:DM], cut(PT, slice(None), p, slice(t * P, (t + 1) * P)),
                                       cut(N, slice(None), p), start=(p == 0), stop=(p == HP - 1))
                    last.then_inc(s.o, 1)

            def attention0():
                s = at[0]

                def query_weights(w):
                    for c in range(NCH):
                        for a in range(2):
                            last = nc.tensor.matmul(psum[c][:, a * DQ:(a + 1) * DQ],
                                                    w[:, WQ0 + a * DM + c * P:WQ0 + a * DM + (c + 1) * P],
                                                    w[:, WCQ0 + a * DQ:WCQ0 + (a + 1) * DQ], start=True, stop=True)
                        last.then_inc(s.a, 1)

                def query_latents(h, banks=range(3)):
                    for j in banks:
                        chunk = (0, 2, 1)[j]
                        for c in range(NCH):
                            last = product(psum[3 * h + j][:, :],
                                           cut(A, slice(None), c, slice(chunk * P, (chunk + 1) * P)),
                                           cut(xs, slice(None), c, slice(h * HALF, (h + 1) * HALF)),
                                           start=(c == 0), stop=(c == NCH - 1))
                        last.then_inc(s.q, 1)

                def body(i, u, count, first=False, final=False):
                    w = W[u]
                    if first:
                        bridge(4, 4)
                        pe.wait_ge(ln[0].lo, 2)
                        pe.wait_ge(s.a_ev, 2)
                        query_latents(0, (0, 1))
                        transpose_tiles(0, 1, (6, 7))
                        query_latents(0, (2,))
                        bridge(3, 4)
                        pe.wait_ge(s.wp_ev, 1)
                        pe.wait_ge(s.n_ev, 1)
                        pe.wait_ge(ln[0].lo, 4)
                    else:
                        pe.wait_ge(s.a_ev, 2 * i + 2)
                        pe.wait_ge(s.wp_ev, i)
                        pe.wait_ge(s.n_ev, i)
                        query_latents(0)
                        pe.wait_ge(s.g_ev, 2 * i)
                    query_latents(1)
                    if not first:
                        transposes(s, i - 1, (6, 7))
                    if not final:
                        pe.wait_ge(s.q_ev, 6 * i + 2)
                        pe.wait_ge(s.w[1 - u], 16 * (count + u))
                        query_weights(W[1 - u])
                    pe.wait_ge(s.q_ev, 6 * i + 4)
                    if not first:
                        score_weights(s, w, 3, WQR0, WKR0, P)
                        pe.wait_ge(s.wo[u], 16 * count)
                        out_weights(s, w, 2, WO0, WCK0)
                    pe.wait_ge(s.wp_ev, i + 1)
                    for h in range(2):
                        pe.wait_ge(s.q_ev, 6 * i + 5 + h)
                        for k, rows in enumerate((qc, qs, qb)):
                            for a in range(2):
                                last = nc.tensor.matmul(psum[4 + h][a * DC:(a + 1) * DC, :],
                                                        Wp[:, k, a * DC:(a + 1) * DC],
                                                        rows[:, a, h * HALF:(h + 1) * HALF],
                                                        start=(k == 0), stop=(k == 2))
                        last.then_inc(s.g, 1)
                    if first:
                        pe.wait_ge(kbd_ready, 1)
                    else:
                        pe.wait_ge(s.t_ev, 2 * i)
                    scores(s, i)

                pe.wait_ge(ident_loaded, 16)
                bridge(4, 2)
                pe.wait_ge(s.w[0], 16)
                query_weights(W[0])
                transpose_tiles(0, 0, (6, 7))
                score_weights(s, W[0], 3, WQR0, WKR0, P)
                pe.wait_ge(s.wo[0], 16)
                out_weights(s, W[0], 5, WO0, WCK0)
                body(0, 0, 1, first=True)
                with pe.Fori(0, HP // 2 - 1) as j:
                    body(2 * j + 1, 1, j + 1)
                    body(2 * j + 2, 0, j + 2)
                body(HP - 1, 1, HP // 2, final=True)
                context_and_output(s, 1)

            def attention1():
                s = at[1]

                def queries(i, h):
                    for c in range(NCH):
                        last = product(psum[4 + h][:, :], cut(M, slice(None), c),
                                       cut(xs, slice(None), c, slice(h * HALF, (h + 1) * HALF)), start=(c == 0), stop=(c == NCH - 1))
                    last.then_inc(s.g, 1)

                def body(i, u, count, first=False, final=False):
                    w = W[u]
                    if not final:
                        pe.wait_ge(s.w[1 - u], 16 * (count + u))
                        if not first:
                            pe.wait_ge(s.n_ev, i)
                        score_weights(s, W[1 - u], 2, WQR1, WKR1, QH)
                    pe.wait_ge(s.m_ev, i + 1)
                    if first:
                        bridge(8, 5)
                        pe.wait_ge(ln[2].lo, 2)
                    else:
                        pe.wait_ge(s.g_ev, 2 * i)
                    queries(i, 0)
                    if first:
                        transpose_tiles(2, 1, (6, 7))
                        bridge(7, 5)
                        pe.wait_ge(ln[2].lo, 4)
                    queries(i, 1)
                    if not final:
                        pe.wait_ge(s.wp_ev, i + 2)
                        t1(W[1 - u], 3)
                    pe.wait_ge(s.wo[u], 16 * count)
                    out_weights(s, w, 2, WO1, WCK1)
                    if not first:
                        transposes(s, i - 1, (0, 1))
                    if not final:
                        pe.wait_ge(s.t1_ev, i + 2)
                        m(W[1 - u], 3)
                    scores(s, i)

                body(0, 0, 1, first=True)
                with pe.Fori(0, HP // 2 - 1) as j:
                    body(2 * j + 1, 1, j + 1)
                    body(2 * j + 2, 0, j + 2)
                body(HP - 1, 1, HP // 2, final=True)
                context_and_output(s, 3)

            def t1(w, bank):
                for a in range(2):
                    for c in range(2):
                        last = nc.tensor.matmul(psum[bank][:, a * DC:(a + 1) * DC],
                                                w[0:QH, WCQ1 + (2 * a + c) * K:WCQ1 + (2 * a + c + 1) * K],
                                                Wp[0:QH, c, a * DC:(a + 1) * DC],
                                                start=(c == 0), stop=(c == 1))
                last.then_inc(at[1].t1, 1)

            def m(w, bank):
                for c in range(NCH):
                    for a in range(2):
                        last = nc.tensor.matmul(psum[bank][:, (2 * c + a) * DC:(2 * c + a + 1) * DC],
                                                w[:, WQ1 + a * DM + c * P:WQ1 + a * DM + (c + 1) * P],
                                                T1[:, a * DC:(a + 1) * DC], start=True, stop=True)
                last.then_inc(at[1].m, 1)

            def first_query_weights(t):
                s = at[1]
                if t == 0:
                    pe.wait_ge(s.w[0], 16)
                    pe.wait_ge(ff[0].hid, 2 * EXPERTS[0] - 1)
                    score_weights(s, W[0], 0, WQR1, WKR1, QH)
                elif t == 4:
                    pe.wait_ge(s.wp_ev, 1)
                    t1(W[0], 1)
                elif t == NT:
                    pe.wait_ge(s.t1_ev, 1)
                    m(W[0], 1)

            def experts(n):
                s, ne = ff[n], EXPERTS[n]
                nr = (E0, E1)[n]
                l = ln[2 * n + 1]

                def gate_up(k, u, h, pair, first=False):
                    if not first:
                        pe.wait_ge(s.hid, k - 1)
                    tk = slice(h * HALF, (h + 1) * HALF)
                    for m in range(2):
                        for c in range(NCH):
                            col = (2 * m + c) * INTER
                            last = product(psum[2 * pair + m][:, :], cut(WG[u], slice(None), slice(col, col + INTER)),
                                           cut(xs, slice(None), c, tk), start=(c == 0), stop=(c == NCH - 1))
                        last.then_inc(s.gu, 1)

                def both(i, u):
                    pe.wait_ge(s.wg, i + 1)
                    gate_up(2 * i, u, 0, 0)
                    gate_up(2 * i + 1, u, 1, 1)

                def down(i, u, first=False, meanwhile=None):
                    pe.wait_ge(s.wd, i + 1)
                    for t in range(NT):
                        if meanwhile:
                            meanwhile(t)
                        if t % 4 == 0:
                            pe.wait_ge(s.h, 1 + t // 2 if first else 2 * i + t // 4 + 1)
                        if t % 2 == 0 and not first:
                            pe.wait_ge(s.x, NT * (i - 1) + t + 2)
                        last = product(psum[4 + t // 2][:, (t % 2) * DM:(t % 2 + 1) * DM],
                                       cut(hT[u], slice(None), slice(t * P, (t + 1) * P)), cut(WD[u], slice(None)))
                        if t % 2:
                            last.then_inc(s.d, 1)

                def router(g):
                    pe.wait_ge(l.whole, g + 1)
                    for t in range(4 * g, 4 * g + 4):
                        for c in range(NCH):
                            last = nc.tensor.matmul(psum[4][:, t * nr:(t + 1) * nr], xnT[:, c, t * P:(t + 1) * P],
                                                    wr[n][:, c, :], start=(c == 0), stop=(c == NCH - 1))
                    return last

                pe.wait_ge(s.wg, 1)
                pe.wait_ge(l.lo, 2)
                gate_up(0, 0, 0, 0, first=True)
                pe.wait_ge(s.wg, 2)
                gate_up(1, 1, 0, 1, first=True)
                transpose_tiles(2 * n + 1, 1, (6, 7))
                router(0)
                pe.wait_ge(l.lo, 4)
                gate_up(2, 0, 1, 0)
                router(1).then_inc(s.logits, 1)
                gate_up(3, 1, 1, 1)
                pe.wait_ge(s.read, 1)
                down(0, 0, first=True)
                even = ne % 2 == 0
                with pe.Fori(0, (ne - 2) // 2 - even) as j:
                    both(2 * j + 2, 0)
                    down(2 * j + 1, 1)
                    both(2 * j + 3, 1)
                    down(2 * j + 2, 0)
                if even:
                    both(ne - 2, 0)
                    down(ne - 3, 1)
                u = (ne - 1) % 2
                pe.wait_ge(s.wg, ne)
                gate_up(2 * ne - 2, u, 0, 0)
                down(ne - 2, 1 - u)
                gate_up(2 * ne - 1, u, 1, 1)
                if n == 0:
                    down(ne - 1, u, meanwhile=first_query_weights)
                    first_query_weights(NT)
                else:
                    down(ne - 1, u)

            attention0()
            pe.wait_ge(const_loaded, 16 * 5)
            experts(0)
            bridge(20, 2)
            transpose_tiles(2, 0, (0, 1))
            attention1()
            experts(1)

        @block.scalar
        def _(act):
            def copy(dst, src):
                return nc.scalar.activation(dst, src, ACT.Copy)

            def normalise(n, g):
                act.wait_ge(ln[n].rstd, LN_STEPS * (g + 1))
                for t in (4 * g + 2, 4 * g + 3):
                    nc.scalar.activation(xn[:, t, :], X[:, t, :], ACT.Identity, bias=shift[:, t:t + 1],
                                         scale=rstd[:, t:t + 1]).then_inc(ln[n].xn_act, 1)

            def transposed_tiles(n, g, banks):
                for b in range(2):
                    act.wait_ge(ln[n].tp, 2 * g + b + 1)
                    tk = slice((4 * g + 2 * b) * P, (4 * g + 2 * b + 2) * P)
                    src = psum[banks[b]][:].rearrange("p (c k) -> p c k", c=NCH)
                    copy(xs[0][:, :, tk], src).then_inc(ln[n].hi, 1)

            def exps(s, i, h):
                act.wait_ge(s.sub, 2 * i + h + 1)
                part = probs[:, 4 * h:4 * h + 4]
                nc.scalar.activation(part, part, ACT.Exp).then_inc(s.exp, 1)

            def queries(s, i):
                for h in range(2):
                    act.wait_ge(s.g, 2 * i + h + 1)
                    copy(G[:, h * HALF:(h + 1) * HALF], psum[4 + h][:]).then_inc(s.g_ev, 1)

            def transposed(s, i, banks):
                for h in range(2):
                    act.wait_ge(s.t, 2 * i + h + 1)
                    copy(PT[0][:, bass.ds(i, 1), h * HALF:(h + 1) * HALF].rearrange("p a t -> p (a t)"),
                         psum[banks[h]][:]).then_inc(s.t_hi, 1)

            def out_weights(s, i, bank):
                act.wait_ge(s.n, i + 1)
                copy(N[0][:, bass.ds(i, 1), :].rearrange("p a t -> p (a t)"), psum[bank][:, 0:DM]).then_inc(s.n_hi, 1)

            def score_weights(s, i, bank, rows, sets):
                act.wait_ge(s.wp, i + 1)
                copy(Wp[0:rows, 0:sets, :],
                     psum[bank][0:rows, 0:sets * P].rearrange("p (c d) -> p c d", c=sets)).then_inc(s.wp_ev, 1)

            def context(s):
                for b in range(NB):
                    act.wait_ge(s.c, b + 1)
                    copy(PT[0][:, :, b * S:(b + 1) * S],
                         psum[b % 8][:].rearrange("p (h s) -> p h s", h=HP)).then_inc(s.c_hi, 1)

            def gate_up_upper(n, e, u, count):
                act.wait_ge(ff[n].w[u], 16 * count)
                copy(WG[u][0][:], WF[u][:, 0:GU]).then_inc(ff[n].ghi, 1)

            def down_upper(n, u):
                copy(WD[u][0][:], WF[u][:, GU:PACKF]).then_inc(ff[n].dhi, 1)

            def first_experts(n):
                for e in range(2):
                    gate_up_upper(n, e, e, 1)
                    down_upper(n, e)

            def attention0():
                s = at[0]

                def query_weights(i):
                    for c in range(NCH):
                        act.wait_ge(s.a, 2 * i + c + 1)
                        copy(A[0][:, c, :], psum[c][:, 0:2 * DQ]).then_inc(s.a_hi, 1)

                def body(i, first=False, final=False):
                    if not first:
                        exps(s, i - 1, 0)
                        exps(s, i - 1, 1)
                        transposed(s, i - 1, (6, 7))
                    if not final:
                        query_weights(i + 1)
                    if not first:
                        score_weights(s, i, 3, P, 3)
                        out_weights(s, i, 2)
                    if first:
                        act.wait_ge(context_step, ROWS_READY)
                    queries(s, i)

                def context_rows_upper():
                    for half, cols in ((slice(0, L), slice(0, DC)), (slice(L, P), slice(DC, 2 * DC))):
                        for u in range(2):
                            last = copy(vbd[0][half, u * NB // 2:(u + 1) * NB // 2, cols], kv_s[u][half])
                    last.then_inc(vbd_hi, 1)

                normalise(0, 0)
                query_weights(0)
                transposed_tiles(0, 0, (6, 7))
                score_weights(s, 0, 3, P, 3)
                out_weights(s, 0, 5)
                normalise(0, 1)
                transposed_tiles(0, 1, (6, 7))
                act.wait_ge(zeros_ready, 3)
                act.wait_ge(context_step, COLS_READY)
                copy(kbd[0:DC, :, 0:L], kvT_s[0:DC])
                copy(kbd[DC:P, :, L:2 * L], kvT_s[DC:P]).then_inc(kbd_ready, 1)
                body(0, first=True)
                context_rows_upper()
                act.wait_ge(const_loaded, 16 * 5)
                nc.scalar.activation(tgate[:], gate[:], ACT.Tanh).then_inc(gate_ready, 1)
                with act.Fori(1, HP - 1) as i:
                    body(i)
                first_experts(0)
                body(HP - 1, final=True)
                exps(s, HP - 1, 0)
                exps(s, HP - 1, 1)
                transposed(s, HP - 1, (6, 7))
                context(s)

            def t1_and_m(i, which, bank=3):
                s = at[1]
                if which == 0:
                    act.wait_ge(s.t1, i + 1)
                    copy(T1[:], psum[bank][:, 0:2 * DC]).then_inc(s.t1_ev, 1)
                else:
                    act.wait_ge(s.m, i + 1)
                    copy(M[0], psum[bank][:, 0:4 * DC].rearrange("p (c r) -> p c r", c=NCH)).then_inc(s.m_hi, 1)

            def attention1():
                s = at[1]

                def body(i, first=False, final=False):
                    if not final:
                        score_weights(s, i + 1, 2, QH, 2)
                    if not first:
                        exps(s, i - 1, 0)
                        exps(s, i - 1, 1)
                    else:
                        normalise(2, 1)
                        transposed_tiles(2, 1, (6, 7))
                    queries(s, i)
                    if not final:
                        t1_and_m(i + 1, 0)
                    out_weights(s, i, 2)
                    if not first:
                        transposed(s, i - 1, (0, 1))
                    if not final:
                        t1_and_m(i + 1, 1)

                body(0, first=True)
                with act.Fori(1, HP - 1) as i:
                    body(i)
                first_experts(1)
                body(HP - 1, final=True)
                exps(s, HP - 1, 0)
                exps(s, HP - 1, 1)
                transposed(s, HP - 1, (6, 7))
                context(s)

            def experts(n):
                s = ff[n]
                nr = (E0, E1)[n]

                def gates(k, pair, first=False):
                    act.wait_ge(s.gu, 2 * k + 1)
                    if not first:
                        act.wait_ge(s.hid, k - 1)
                    nc.scalar.activation(silu[:, pair, :], psum[2 * pair][:], ACT.Tanh, scale=0.5).then_inc(s.tanh, 1)

                def hidden_upper(k, u, h, pair):
                    act.wait_ge(s.hid, k + 1)
                    copy(hT[u][0][:, h * HALF:(h + 1) * HALF], hid[:, pair, :]).then_inc(s.hhi, 1)

                def start():
                    gates(0, 0, first=True)
                    normalise(2 * n + 1, 1)
                    gates(1, 1, first=True)
                    transposed_tiles(2 * n + 1, 1, (6, 7))
                    hidden_upper(0, 0, 0, 0)
                    hidden_upper(1, 1, 0, 1)
                    gates(2, 0)
                    hidden_upper(2, 0, 1, 0)
                    act.wait_ge(s.gu, 6)
                    gate_up_upper(n, 2, 0, 2)
                    act.wait_ge(s.route, 1)
                    nc.scalar.activation(rt[0][:, :, 0:nr], rt[0][:, :, 0:nr], ACT.Exp).then_inc(s.rexp, 1)
                    gates(3, 1)
                    act.wait_ge(s.gu, 8)
                    gate_up_upper(n, 3, 1, 2)
                    hidden_upper(3, 1, 1, 1)
                    act.wait_ge(s.d, NT // 2)
                    down_upper(n, 0)

                def body(i, u, count, gu=True, d=True, last=False):
                    gates(2 * i, 0)
                    if last:
                        hidden_upper(2 * i, u, 0, 0)
                    gates(2 * i + 1, 1)
                    if not last:
                        hidden_upper(2 * i, u, 0, 0)
                    elif n == 0:
                        score_weights(at[1], 0, 0, QH, 2)
                    hidden_upper(2 * i + 1, u, 1, 1)
                    if gu:
                        act.wait_ge(s.gu, 4 * i + 4)
                        gate_up_upper(n, i + 2, u, count)
                    if d:
                        act.wait_ge(s.d, NT // 2 * i)
                        down_upper(n, 1 - u)

                ne = EXPERTS[n]
                normalise(2 * n + 1, 0)
                transposed_tiles(2 * n + 1, 0, (0, 1))
                start()
                pairs = (ne - 4) // 2
                with act.Fori(0, pairs) as j:
                    body(2 * j + 2, 0, j + 3)
                    body(2 * j + 3, 1, j + 3)
                for i in range(2 * pairs + 2, ne):
                    body(i, i % 2, i // 2 + 2, gu=i + 2 < ne, d=i + 1 < ne,
                         last=i == ne - 1)

            attention0()
            experts(0)
            t1_and_m(0, 0, 1)
            t1_and_m(0, 1, 1)
            normalise(2, 0)
            transposed_tiles(2, 0, (0, 1))
            attention1()
            experts(1)

        @block.vector
        def _(dve):
            V = nc.vector

            def statistics(n, t):
                V.bn_stats(stats[:, t, :], X[:, t, :]).then_inc(ln[n].stat, 1)

            def normalise(n, g, arrived=None, lower=None, lower_at=None, meanwhile=None):
                s, tiles = ln[n], range(4 * g, 4 * g + 4)
                for t in tiles if arrived else ():
                    if t == lower_at:
                        lower()
                    arrived(t)
                    statistics(n, t)
                for t in tiles:
                    dve.wait_ge(s.stat, t + 1)
                    V.bn_aggr(meanvar[:, t, :], stats[:, t, :]).then_inc(s.rstd, 1)
                if lower and lower_at is None:
                    lower()
                dve.wait_ge(s.rstd, LN_STEPS * g + 4)
                count = [LN_STEPS * g + 4]

                def link(op):
                    count[0] += 1
                    op.then_inc(s.rstd, 1)
                    if meanwhile:
                        meanwhile(count[0] - LN_STEPS * g - 5)
                    dve.wait_ge(s.rstd, count[0])

                y, v, w = (r[:, 4 * g:4 * g + 4] for r in (rstd, varep, newton))
                link(V.tensor_scalar(v, meanvar[:, 4 * g:4 * g + 4, 1], EPS_LN, None, ALU.add))
                link(V.tensor_scalar(y.bitcast(I32), v.bitcast(I32), 1, None, ALU.arith_shift_right))
                link(V.tensor_scalar(y.bitcast(I32), y.bitcast(I32), -1.0, float(RSQRT_GUESS), ALU.mult, ALU.add))
                for _ in range(3):
                    link(V.scalar_tensor_tensor(w, y, -0.5, y, ALU.mult, ALU.mult))
                    link(V.tensor_tensor(w, w, v, ALU.mult))
                    link(V.scalar_tensor_tensor(y, w, 1.5, y, ALU.add, ALU.mult))
                V.scalar_tensor_tensor(shift[:, 4 * g:4 * g + 4], meanvar[:, 4 * g:4 * g + 4, 0], -1.0, y,
                                       ALU.mult, ALU.mult).then_inc(s.rstd, 1)
                assert count[0] + 1 == LN_STEPS * (g + 1)
                for t in tiles[0:2]:
                    V.tensor_scalar(xn[:, t, :], X[:, t, :], meanvar[:, t, 0:1], rstd[:, t:t + 1],
                                    ALU.subtract, ALU.mult).then_inc(s.xn, 1)

            def lower_part(n, g, banks, parts=range(2)):
                for b in parts:
                    dve.wait_ge(ln[n].hi, 2 * g + b + 1)
                    tk = slice((4 * g + 2 * b) * P, (4 * g + 2 * b + 2) * P)
                    V.tensor_tensor(xs[1][:, :, tk], psum[banks[b]][:].rearrange("p (c k) -> p c k", c=NCH),
                                    xs[0][:, :, tk].bitcast(F32), ALU.subtract).then_inc(ln[n].lo, 1)

            def layer_norm(n, arrived, banks, lower_at=None):
                normalise(n, 0, arrived)
                normalise(n, 1, arrived, lambda: lower_part(n, 0, banks), lower_at)

            def lower(dst, src, upper, done):
                V.tensor_tensor(dst, src, upper.bitcast(F32), ALU.subtract).then_inc(done, 1)

            def transposed_lower(s, i, banks):
                for h in range(2):
                    dve.wait_ge(s.t_hi, 2 * i + h + 1)
                    hi, lo = (part[:, bass.ds(i, 1), h * HALF:(h + 1) * HALF].rearrange("p a t -> p (a t)")
                              for part in PT)
                    lower(lo, psum[banks[h]][:], hi, s.t_ev)

            def out_weights_lower(s, i, bank):
                dve.wait_ge(s.n_hi, i + 1)
                hi, lo = (part[:, bass.ds(i, 1), :].rearrange("p a t -> p (a t)") for part in N)
                lower(lo, psum[bank][:, 0:DM], hi, s.n_ev)

            def context_lower(s):
                for b in range(NB):
                    dve.wait_ge(s.c_hi, b + 1)
                    hi, lo = (part[:, :, b * S:(b + 1) * S] for part in PT)
                    lower(lo, psum[b % 8][:].rearrange("p (h s) -> p h s", h=HP), hi, s.c_ev)

            def softmax_shift(s, i):
                for h in range(2):
                    dve.wait_ge(s.s, 2 * i + h + 1)
                    sc = psum[6 + h][:].rearrange("p (t a l) -> p t a l", t=4, a=2)
                    mx = rowmax[:, 4 * h:4 * h + 4, :]
                    V.tensor_reduce(mx, sc, AX, ALU.max).then_inc(s.max, 1)
                    dve.wait_ge(s.max, 2 * i + h + 1)
                    V.tensor_tensor(probs[:, 4 * h:4 * h + 4], sc, mx.unsqueeze(3).to_broadcast([P, 4, 2, L]),
                                    ALU.subtract).then_inc(s.sub, 1)

            def softmax_sums(s, i, normalise=False):
                for h in range(2):
                    part, rec = probs[:, 4 * h:4 * h + 4], rowrec[:, 4 * h:4 * h + 4, :]
                    dve.wait_ge(s.exp, 2 * i + h + 1)
                    V.tensor_reduce(rowsum[:, 4 * h:4 * h + 4, :], part, AX, ALU.add).then_inc(s.sum, 1)
                    dve.wait_ge(s.sum, 2 * i + h + 1)
                    V.reciprocal(rec, rowsum[:, 4 * h:4 * h + 4, :]).then_inc(s.rec, 1)
                    if normalise:
                        dve.wait_ge(s.rec, 2 * i + h + 1)
                        V.tensor_tensor(part, part, rec.unsqueeze(3).to_broadcast([P, 4, 2, L]),
                                        ALU.mult).then_inc(s.p, 1)

            def add_output(s, g, t):
                dve.wait_ge(s.o, t + 1)
                V.scalar_tensor_tensor(X[:, t, :], psum[t][:, 0:DM], tgate[:, g:g + 1], X[:, t, :],
                                       ALU.mult, ALU.add).then_inc(s.x, 1)
                dve.wait_ge(s.x, t + 1)

            def query_weights_lower(i, chunks=range(NCH)):
                for c in chunks:
                    dve.wait_ge(at[0].a_hi, 2 * i + c + 1)
                    V.tensor_tensor(A[1][:, c, :], psum[c][:, 0:2 * DQ], A[0][:, c, :].bitcast(F32),
                                    ALU.subtract).then_inc(at[0].a_ev, 1)

            def attention0():
                s = at[0]

                def rope(i, n):
                    h, j = divmod(n, 3)
                    dve.wait_ge(s.q, 6 * i + n + 1)
                    tk = slice(h * HALF, (h + 1) * HALF)

                    def times(dst, half, tbl):
                        return V.tensor_tensor(dst.rearrange("p (b s) -> p b s", s=S),
                                               psum[n][half, :].rearrange("p (b s) -> p b s", s=S),
                                               tbl[half, j, :].unsqueeze(1).to_broadcast([dst.shape[0], HALF // S, S]),
                                               ALU.mult)

                    if j < 2:
                        times(qc[:, j, tk], slice(0, P), cosQ_s)
                        last = times(qs[:, j, tk], slice(0, P), sinQ_s)
                    else:
                        for a in range(2):
                            src = slice(a * S, (a + 1) * S)
                            times(qb[0:S, a, tk], src, cosQ_s)
                            last = times(qb[S:P, a, tk], src, sinQ_s)
                    last.then_inc(s.q_ev, 1)

                def body(i, first=False, final=False):
                    if not first:
                        softmax_shift(s, i - 1)
                        rope(i, 0)
                        softmax_sums(s, i - 1)
                        rope(i, 1)
                    rope(i, 2)
                    for n in range(3, 6):
                        rope(i, n)
                    if not first:
                        transposed_lower(s, i - 1, (6, 7))
                    if not final:
                        query_weights_lower(i + 1)
                    if not first:
                        out_weights_lower(s, i, 2)

                dve.wait_ge(query_rope_loaded, 16 * 2)
                rope(0, 0)
                rope(0, 1)
                lower_part(0, 1, (6, 7))
                body(0, first=True)
                with dve.Fori(1, HP - 1) as i:
                    body(i)
                body(HP - 1, final=True)
                softmax_shift(s, HP - 1)
                softmax_sums(s, HP - 1, normalise=True)
                transposed_lower(s, HP - 1, (6, 7))
                context_lower(s)

            def m_lower(i, bank=3):
                s = at[1]
                dve.wait_ge(s.m_hi, i + 1)
                V.tensor_tensor(M[1], psum[bank][:, 0:4 * DC].rearrange("p (c r) -> p c r", c=NCH),
                                M[0].bitcast(F32), ALU.subtract).then_inc(s.m_ev, 1)

            def attention1():
                s = at[1]

                def body(i, final=False):
                    softmax_shift(s, i)
                    softmax_sums(s, i)
                    out_weights_lower(s, i + 1, 2)
                    transposed_lower(s, i, (0, 1))
                    if not final:
                        m_lower(i + 2)

                out_weights_lower(s, 0, 2)
                m_lower(1)
                with dve.Fori(0, HP - 2) as i:
                    body(i)
                body(HP - 2, final=True)
                softmax_shift(s, HP - 1)
                softmax_sums(s, HP - 1, normalise=True)
                transposed_lower(s, HP - 1, (6, 7))
                context_lower(s)

            def logits(n):
                s, nr = ff[n], (E0, E1)[n]
                dve.wait_ge(s.logits, 1)
                lg = psum[4][:, 0:NT * nr].rearrange("p (t e) -> p t e", e=nr)
                dst = rt[0][:, :, 0:nr]
                if n:
                    op = V.tensor_tensor(dst, lg, bias_s[:, 0:nr].unsqueeze(1).to_broadcast([P, NT, nr]), ALU.add)
                else:
                    op = V.tensor_copy(dst, lg)
                op.then_inc(s.read, 1)

            route_step, route_steps = sem("route_step"), [0]

            class Routing:

                def __init__(r, n):
                    r.n, r.nr, r.g = n, (E0, E1)[n], 2 + n
                    r.a, r.b, r.c, r.d = (t[:, :, 0:r.nr] for t in rt)

                def link(r, op):
                    route_steps[0] += 1
                    op.then_inc(route_step, 1)
                    dve.wait_ge(route_step, route_steps[0])

                def by_expert(r, v):
                    return v[:].unsqueeze(2).to_broadcast([P, NT, r.nr])

                def numbers(r):
                    return iota[:, 0:r.nr].unsqueeze(1).to_broadcast([P, NT, r.nr])

                def softmax(r):
                    a, s, mx, den = r.a, ff[r.n], rs[0], rs[4]
                    dve.wait_ge(s.read, 1)
                    r.link(V.tensor_reduce(mx[:], a, AX, ALU.max))
                    V.tensor_tensor(a, a, r.by_expert(mx), ALU.subtract).then_inc(s.route, 1)
                    dve.wait_ge(s.rexp, 1)
                    r.link(V.tensor_reduce(den[:], a, AX, ALU.add))
                    r.link(V.reciprocal(den[:], den[:]))
                    r.link(V.tensor_tensor(a, a, r.by_expert(den), ALU.mult))

                def largest(r, k):
                    a, b, dst, mx, idx = r.a, r.b, (r.c, r.d)[k], rs[k], rs[2 + k]
                    r.link(V.tensor_reduce(mx[:], a, AX, ALU.max))
                    r.link(V.tensor_tensor(b, a, r.by_expert(mx), ALU.is_lt))
                    r.link(V.scalar_tensor_tensor(b, b, float(E1), r.numbers(), ALU.mult, ALU.add))
                    r.link(V.tensor_reduce(idx[:], b, AX, ALU.min))
                    r.link(V.tensor_tensor(dst, r.numbers(), r.by_expert(idx), ALU.is_equal))
                    if k == 0:
                        r.link(V.scalar_tensor_tensor(a, dst, -BIG, a, ALU.mult, ALU.add))

                def weights(r):
                    n, nr, g, c, d = r.n, r.nr, r.g, r.c, r.d
                    m1, m2, den = rs[0], rs[1], rs[4]
                    V.tensor_tensor(c, c, r.by_expert(m1), ALU.mult)
                    V.tensor_tensor(den[:], m1[:], m2[:], ALU.add)
                    r.link(V.tensor_tensor(d, d, r.by_expert(m2), ALU.mult))
                    if n:
                        r.link(V.tensor_scalar(den[:], den[:], EPS_TOPK, None, ALU.add))
                    r.link(V.reciprocal(den[:], den[:]))
                    r.link(V.tensor_scalar(den[:], den[:], tgate[:, g:g + 1], None, ALU.mult))
                    if n:
                        r.link(V.tensor_scalar(coef[:, :, nr], coef[:, :, nr], tgate[:, g:g + 1], None, ALU.mult))
                    r.link(V.tensor_tensor(c, c, d, ALU.add))
                    r.link(V.tensor_tensor(coef[:, :, 0:nr], c, r.by_expert(den), ALU.mult))

            def expert_add(n, i, t):
                s = ff[n]
                dve.wait_ge(s.d, NT // 2 * i + t // 2 + 1)
                if not isinstance(i, int) or i > 0:
                    dve.wait_ge(s.x, NT * (i - 1) + t + 1)
                V.scalar_tensor_tensor(X[:, t, :], psum[4 + t // 2][:, (t % 2) * DM:(t % 2 + 1) * DM],
                                       coef[:, t, bass.ds(i, 1)], X[:, t, :], ALU.mult, ALU.add).then_inc(s.x, 1)

            def experts(n):
                s, ne = ff[n], EXPERTS[n]

                def hidden_values(k, pair, first=False):
                    dve.wait_ge(s.gu, 2 * k + 2)
                    dve.wait_ge(s.tanh, k + 1)
                    V.scalar_tensor_tensor(silu[:, pair, :], silu[:, pair, :], 1.0, psum[2 * pair][:], ALU.add,
                                           ALU.mult).then_inc(s.silu, 1)
                    dve.wait_ge(s.silu, k + 1)
                    if not first:
                        dve.wait_ge(s.h, k - 1)
                    V.scalar_tensor_tensor(hid[:, pair, :], silu[:, pair, :], 0.5, psum[2 * pair + 1][:], ALU.mult,
                                           ALU.mult).then_inc(s.hid, 1)

                def hidden(i):
                    hidden_values(2 * i, 0)
                    hidden_values(2 * i + 1, 1)

                def add(i):
                    for t in range(NT):
                        expert_add(n, i, t)

                hidden_values(0, 0, first=True)
                lower_part(2 * n + 1, 1, (6, 7))
                hidden_values(1, 1, first=True)
                hidden_values(2, 0)
                logits(n)
                route = Routing(n)
                route.softmax()
                route.largest(0)
                hidden_values(3, 1)
                route.largest(1)
                route.weights()
                add(0)
                even = ne % 2 == 0
                with dve.Fori(0, (ne - 2) // 2 - even) as j:
                    for k in range(2):
                        hidden(2 * j + 2 + k)
                        add(2 * j + 1 + k)
                if even:
                    hidden(ne - 2)
                    add(ne - 3)
                hidden_values(2 * ne - 2, 0)
                for t in range(6):
                    expert_add(n, ne - 2, t)
                hidden_values(2 * ne - 1, 1)
                for t in range(6, NT):
                    expert_add(n, ne - 2, t)
                dve.wait_ge(s.h, 2 * ne - 1)
                dve.wait_ge(s.hhi, 2 * ne)
                u = (ne - 1) % 2
                V.tensor_tensor(hT[u][1][:, HALF:2 * HALF], hid[:, 1, :], hT[u][0][:, HALF:2 * HALF].bitcast(F32),
                                ALU.subtract).then_inc(s.h, 1)

            def arrived(t):
                dve.wait_ge(x_loaded[t // 2], 16)

            def first_lower_parts(k):
                if k < 2:
                    query_weights_lower(0, [k])
                elif k < 4:
                    lower_part(0, 0, (6, 7), [k - 2])
                elif k == 8:
                    out_weights_lower(at[0], 0, 5)

            normalise(0, 0, arrived)
            normalise(0, 1, arrived, meanwhile=first_lower_parts)
            attention0()
            dve.wait_ge(gate_ready, 1)
            dve.wait_ge(zeros_ready, 4)
            layer_norm(1, lambda t: add_output(at[0], 0, t), (0, 1), lower_at=NT - 1)
            experts(0)

            def second_group(k):
                if k < 4:
                    expert_add(0, EXPERTS[0] - 1, 4 + k)
                elif k == 4:
                    m_lower(0, 1)

            def all_added(t):
                dve.wait_ge(ff[0].x, NT * (EXPERTS[0] - 1) + t + 1)

            def first_group_lower(k):
                if k == 5:
                    lower_part(2, 0, (0, 1), [0])
                elif k == 9:
                    lower_part(2, 0, (0, 1), [1])

            for t in range(5):
                if t < 4:
                    expert_add(0, EXPERTS[0] - 1, t)
                if t > 0:
                    all_added(t - 1)
                    statistics(2, t - 1)
            normalise(2, 0, meanwhile=second_group)
            normalise(2, 1, all_added, meanwhile=first_group_lower)
            lower_part(2, 1, (6, 7))
            attention1()
            layer_norm(3, lambda t: add_output(at[1], 1, t), (0, 1), lower_at=NT - 1)
            experts(1)
            for t in range(NT):
                expert_add(1, EXPERTS[1] - 1, t)


def rope_tables(length, dim):
    inv = (1.0 / 10000.0 ** (np.arange(0, dim, 2, dtype=np.float32) / np.float32(dim))).astype(np.float32)
    f = np.arange(length, dtype=np.float32)[:, None] * inv[None, :]
    return np.repeat(np.sin(f), 2, axis=-1), np.repeat(np.cos(f), 2, axis=-1)


def layouts(a):
    f = {k: np.asarray(v) for k, v in a.items()}
    d = {"x": f["x"].reshape(TOK, DM)}
    ctx = f["ctx_512"]
    kvT = np.transpose(ctx, (2, 0, 1)).reshape(DC, TOK)
    hd = DC // 2
    d["kvT"] = np.concatenate([kvT, kvT])
    rot = np.concatenate([kvT[hd:], kvT[:hd]])
    d["kvTrot"] = np.concatenate([rot, rot])
    kv = np.transpose(ctx, (1, 0, 2)).reshape(L, NB * DC)
    d["kv"] = np.concatenate([kv, kv])
    sin, cos = rope_tables(L, DC)
    sign = np.where(np.arange(DC) < hd, -1.0, 1.0).astype(np.float32)
    d["cosT"] = np.concatenate([cos.T, cos.T])
    d["sinT"] = np.concatenate([(sin * sign).T] * 2)
    d["cosR"] = np.concatenate([cos, cos])
    d["sinR"] = np.concatenate([sin * sign] * 2)
    sin, cos = rope_tables(S, DQ)
    half = DQ // 2
    to = (np.arange(DQ) + half) % DQ
    sg = np.where(np.arange(DQ) < half, 1.0, -1.0).astype(np.float32)
    sinp = (sin[:, to] * sg).T
    cosp = cos.T
    stack = lambda m: np.stack([m[0:P], m[DQ - P:DQ], np.concatenate([m[P:DQ], m[0:DQ - P]])], axis=1)
    d["cosQ"], d["sinQ"] = stack(cosp), stack(sinp)

    def pairs(w):
        return w.reshape(HP, 2, *w.shape[1:])

    for n in range(2):
        g = lambda k: f[f"L{n}_xattn_{k}"]
        wq = pairs(g("Wq").reshape(H, K, DM))
        wcq, wck = pairs(g("w_kc_q")), pairs(g("w_kc_kv"))
        wqr, wkr = pairs(g("W_qr")), pairs(g("W_kr"))
        wo = pairs(np.transpose(g("Wo").reshape(DM, H, K), (1, 2, 0)))
        side = lambda w: np.transpose(w, (0, 2, 1, 3)).reshape(HP, w.shape[2], -1)
        kr = np.zeros((HP, 2, R, 2, DC), np.float32)
        for a in range(2):
            kr[:, a, :, a] = np.transpose(wkr[:, a], (0, 2, 1))
        kr = kr.reshape(HP, P, P)
        rt = lambda w: np.transpose(w, (0, 1, 3, 2)).reshape(HP, P, -1)
        if n == 0:
            own = lambda w: rt(np.stack([w[:, 0, 0:P], w[:, 1, DQ - P:DQ]], axis=1))
            shared = lambda w: rt(np.stack([w[:, 0, P:DQ], w[:, 1, 0:DQ - P]], axis=1))
            wqrs = wqr[:, :, to]
            qr = [own(wqr), own(wqrs), shared(wqr), shared(wqrs)]
            cols = [side(wq), side(wcq), *qr, kr, side(wo), side(wck)]
        else:
            chunks = np.zeros((HP, P, 2, 2, K), np.float32)
            chunks[:, 0:QH] = np.transpose(wcq.reshape(HP, 2, K, 2, QH), (0, 4, 1, 3, 2))
            cols = [side(wq), chunks.reshape(HP, P, -1), rt(wqr), kr, side(wo), side(wck)]
        d[f"attn{n}"] = np.concatenate(cols, axis=2)

    def expert_pack(wg, wu, wd):
        e = wg.shape[0]
        chunk = lambda w: np.transpose(w.reshape(e, NCH, P, INTER), (0, 2, 1, 3)).reshape(e, P, -1)
        return np.concatenate([chunk(wg), chunk(wu), wd], axis=2)

    gu = f["L0_ffn_expert_gate_up"]
    d["ffn0"] = expert_pack(gu[:, :, 0::2], gu[:, :, 1::2], f["L0_ffn_expert_down"])
    d["ffn1"] = expert_pack(*(np.concatenate([f[f"L1_ffn_{k}"], f[f"L1_ffn_s{k}"][None]]) for k in ("Wg", "Wu", "Wd")))
    router = lambda w: np.transpose(w.T.reshape(NCH, P, -1), (1, 0, 2))
    d["router0"], d["router1"] = router(f["L0_ffn_router_gate"]), router(f["L1_ffn_Wr"])
    rows = lambda v: np.broadcast_to(v[None], (P, v.shape[0]))
    d["bias1"] = rows(f["L1_ffn_bias"])
    d["gates"] = rows(np.concatenate([f["g_xattn"], f["g_ffn"]]))
    d["ident_d"] = np.eye(P, dtype=np.float32)
    d["iota_d"] = rows(np.arange(E1, dtype=np.float32))
    return {k: np.ascontiguousarray(v, dtype=np.float32) for k, v in d.items()}


def kernel(**inputs):
    import concourse.bacc as bacc
    from concourse.bass_utils import run_bass_kernel_spmd

    nc = bacc.Bacc("TRN2", target_bir_lowering=False, num_devices=1)
    arrays = layouts(inputs)
    aps = {k: nc.dram_tensor(k, v.shape, F32, kind="ExternalInput").ap() for k, v in arrays.items()}
    out = nc.dram_tensor("out", (TOK, DM), F32, kind="ExternalOutput").ap()
    build(nc, out=out, **aps)
    r = run_bass_kernel_spmd(nc, [arrays], core_ids=[0])
    return r.results[0]["out"].reshape(NB, S, DM)
```
